# Optimizing a Trainium2 kernel written in Bass

```python
import numpy as np
import jax
import jax.numpy as jnp

def _softmax(x, axis=-1):
    return jax.nn.softmax(x, axis=axis)

def _gelu(x):
    return jax.nn.gelu(x, approximate=True)

def _silu(x):
    return jax.nn.silu(x)

def _sigmoid(x):
    return jax.nn.sigmoid(x)

def _layernorm(x, axis=-1, eps=1e-05):
    m = jnp.mean(x, axis=axis, keepdims=True)
    v = jnp.var(x, axis=axis, keepdims=True)
    return (x - m) / jnp.sqrt(v + eps)

def _scatter_add(tgt, idx, src, axis=0):
    return tgt.at[idx].add(src)

def _segment_sum(src, seg, n):
    return jax.ops.segment_sum(src, seg, n)
kernel_name = 'mk_seq_postln_d1_jaxref_r4_b9ac87'

def setup_inputs(seed: int=0):
    np.random.seed(seed)
    _w = jnp.asarray

    def _L0_attn_setup():
        import jax, jax.numpy as jnp
        import numpy as np
        B, T, D, H = (2, 512, 256, 4)
        DK, DV = (256, 512)
        HK, HV = (DK // H, DV // H)
        LR = 16
        EPS = 1e-05
        GATE_NORM = 16.0

        def _xavier(k, shape, gain):
            fan_in, fan_out = shape
            lim = gain * np.sqrt(6.0 / (fan_in + fan_out))
            return jax.random.uniform(k, shape, jnp.float32, -lim, lim)

        def _gla_scan(q, k, v, g):
            S0 = jnp.zeros((q.shape[-1], v.shape[-1]), q.dtype)

            def step(S, inp):
                qt, kt, vt, gt = inp
                S = jnp.exp(gt)[:, None] * S + kt[:, None] * vt[None, :]
                return (S, qt @ S)
            return jax.lax.scan(step, S0, (q, k, v, g))[1]

        def _forward(x, Wq, Wk, Wv, Wg, gk_w1, gk_w2, gk_b, Wo, rms_w):
            b, t = (x.shape[0], x.shape[1])
            scale = HK ** (-0.5)
            q = (x @ Wq).reshape(b, t, H, HK).transpose(0, 2, 1, 3) * scale
            k = (x @ Wk).reshape(b, t, H, HK).transpose(0, 2, 1, 3)
            v = (x @ Wv).reshape(b, t, H, HV).transpose(0, 2, 1, 3)
            gl = x @ gk_w1 @ gk_w2 + gk_b
            g = jax.nn.log_sigmoid(gl.astype(jnp.float32)) / GATE_NORM
            g = g.reshape(b, t, H, HK).transpose(0, 2, 1, 3)
            o = jax.vmap(jax.vmap(_gla_scan))(q, k, v, g)
            o = o.transpose(0, 2, 1, 3)
            o = o * jax.lax.rsqrt(jnp.mean(o * o, axis=-1, keepdims=True) + EPS) * rms_w
            o = o.reshape(b, t, DV) * jax.nn.silu(x @ Wg)
            return o @ Wo
        key = jax.random.key(seed)
        ks = jax.random.split(key, 10)
        g_qkv = 2 ** (-2.5)
        return {'x': jax.random.normal(ks[0], (B, T, D), jnp.float32), 'Wq': _xavier(ks[1], (D, DK), g_qkv), 'Wk': _xavier(ks[2], (D, DK), g_qkv), 'Wv': _xavier(ks[3], (D, DV), g_qkv), 'Wg': _xavier(ks[4], (D, DV), g_qkv), 'gk_w1': _xavier(ks[5], (D, LR), g_qkv), 'gk_w2': _xavier(ks[6], (LR, DK), g_qkv), 'gk_b': jnp.zeros((DK,), jnp.float32), 'Wo': _xavier(ks[7], (DV, D), 2 ** (-1)), 'rms_w': jnp.ones((HV,), jnp.float32)}
    _L0_attn_in = _L0_attn_setup()

    def _L0_ffn_setup():
        import jax, jax.numpy as jnp
        import numpy as np
        D_IN, D_HID = (256, 1024)

        def _ternary(key, shape):
            return jax.random.randint(key, shape, -1, 2).astype(jnp.float32)

        def _tlin(x, w, s):
            return jnp.einsum('bsi,oi->bso', x, w) * s
        key = jax.random.key(seed)
        ks = jax.random.split(key, 12)
        inv = lambda fan: 1.0 / np.sqrt(fan).astype(np.float32)
        return {'x': jax.random.normal(ks[0], (4, 512, D_IN), dtype=jnp.float32), 'w1_w': _ternary(ks[1], (D_HID, D_IN)), 'w1_s': jax.random.uniform(ks[2], (D_HID,), dtype=jnp.float32) * inv(D_IN), 'w2_w': _ternary(ks[3], (D_HID, D_IN)), 'w2_s': jax.random.uniform(ks[4], (D_HID,), dtype=jnp.float32) * inv(D_IN), 'h1_w': _ternary(ks[5], (D_HID, D_HID)), 'h1_s': jax.random.uniform(ks[6], (D_HID,), dtype=jnp.float32) * inv(D_HID), 'h2_w': _ternary(ks[7], (D_HID, D_HID)), 'h2_s': jax.random.uniform(ks[8], (D_HID,), dtype=jnp.float32) * inv(D_HID), 'w3_w': _ternary(ks[9], (D_IN, D_HID)), 'w3_s': jax.random.uniform(ks[10], (D_IN,), dtype=jnp.float32) * inv(D_HID)}
    _L0_ffn_in = _L0_ffn_setup()
    _d = {'L0_attn_x': _L0_attn_in['x'], 'L0_attn_Wq': _L0_attn_in['Wq'], 'L0_attn_Wk': _L0_attn_in['Wk'], 'L0_attn_Wv': _L0_attn_in['Wv'], 'L0_attn_Wg': _L0_attn_in['Wg'], 'L0_attn_gk_w1': _L0_attn_in['gk_w1'], 'L0_attn_gk_w2': _L0_attn_in['gk_w2'], 'L0_attn_gk_b': _L0_attn_in['gk_b'], 'L0_attn_Wo': _L0_attn_in['Wo'], 'L0_attn_rms_w': _L0_attn_in['rms_w'], 'L0_ffn_w1_w': _L0_ffn_in['w1_w'], 'L0_ffn_w1_s': _L0_ffn_in['w1_s'], 'L0_ffn_w2_w': _L0_ffn_in['w2_w'], 'L0_ffn_w2_s': _L0_ffn_in['w2_s'], 'L0_ffn_h1_w': _L0_ffn_in['h1_w'], 'L0_ffn_h1_s': _L0_ffn_in['h1_s'], 'L0_ffn_h2_w': _L0_ffn_in['h2_w'], 'L0_ffn_h2_s': _L0_ffn_in['h2_s'], 'L0_ffn_w3_w': _L0_ffn_in['w3_w'], 'L0_ffn_w3_s': _L0_ffn_in['w3_s']}
    _x0 = _d['L0_attn_x']
    _d['L0_attn_x'] = jax.random.normal(jax.random.fold_in(jax.random.key(seed), 1), (4, 1024, 256), dtype=_x0.dtype)
    del _x0
    return _d

def reference(L0_attn_x, L0_attn_Wq, L0_attn_Wk, L0_attn_Wv, L0_attn_Wg, L0_attn_gk_w1, L0_attn_gk_w2, L0_attn_gk_b, L0_attn_Wo, L0_attn_rms_w, L0_ffn_w1_w, L0_ffn_w1_s, L0_ffn_w2_w, L0_ffn_w2_s, L0_ffn_h1_w, L0_ffn_h1_s, L0_ffn_h2_w, L0_ffn_h2_s, L0_ffn_w3_w, L0_ffn_w3_s):

    def _L0_attn_ref(x, Wq, Wk, Wv, Wg, gk_w1, gk_w2, gk_b, Wo, rms_w):
        import jax, jax.numpy as jnp
        import numpy as np
        B, T, D, H = (2, 512, 256, 4)
        DK, DV = (256, 512)
        HK, HV = (DK // H, DV // H)
        LR = 16
        EPS = 1e-05
        GATE_NORM = 16.0

        def _xavier(k, shape, gain):
            fan_in, fan_out = shape
            lim = gain * np.sqrt(6.0 / (fan_in + fan_out))
            return jax.random.uniform(k, shape, jnp.float32, -lim, lim)

        def _gla_scan(q, k, v, g):
            S0 = jnp.zeros((q.shape[-1], v.shape[-1]), q.dtype)

            def step(S, inp):
                qt, kt, vt, gt = inp
                S = jnp.exp(gt)[:, None] * S + kt[:, None] * vt[None, :]
                return (S, qt @ S)
            return jax.lax.scan(step, S0, (q, k, v, g))[1]

        def _forward(x, Wq, Wk, Wv, Wg, gk_w1, gk_w2, gk_b, Wo, rms_w):
            b, t = (x.shape[0], x.shape[1])
            scale = HK ** (-0.5)
            q = (x @ Wq).reshape(b, t, H, HK).transpose(0, 2, 1, 3) * scale
            k = (x @ Wk).reshape(b, t, H, HK).transpose(0, 2, 1, 3)
            v = (x @ Wv).reshape(b, t, H, HV).transpose(0, 2, 1, 3)
            gl = x @ gk_w1 @ gk_w2 + gk_b
            g = jax.nn.log_sigmoid(gl.astype(jnp.float32)) / GATE_NORM
            g = g.reshape(b, t, H, HK).transpose(0, 2, 1, 3)
            o = jax.vmap(jax.vmap(_gla_scan))(q, k, v, g)
            o = o.transpose(0, 2, 1, 3)
            o = o * jax.lax.rsqrt(jnp.mean(o * o, axis=-1, keepdims=True) + EPS) * rms_w
            o = o.reshape(b, t, DV) * jax.nn.silu(x @ Wg)
            return o @ Wo
        return _forward(x, Wq, Wk, Wv, Wg, gk_w1, gk_w2, gk_b, Wo, rms_w)

    def _L0_ffn_ref(x, w1_w, w1_s, w2_w, w2_s, h1_w, h1_s, h2_w, h2_s, w3_w, w3_s):
        import jax, jax.numpy as jnp
        import numpy as np
        D_IN, D_HID = (256, 1024)

        def _ternary(key, shape):
            return jax.random.randint(key, shape, -1, 2).astype(jnp.float32)

        def _tlin(x, w, s):
            return jnp.einsum('bsi,oi->bso', x, w) * s
        h = jax.nn.silu(_tlin(x, w1_w, w1_s)) * _tlin(x, w2_w, w2_s)
        h = jax.nn.gelu(_tlin(h, h1_w, h1_s), approximate=False)
        h = jax.nn.gelu(_tlin(h, h2_w, h2_s), approximate=False)
        return _tlin(h, w3_w, w3_s)
    x = L0_attn_x
    x = _layernorm(x + _L0_attn_ref(x, L0_attn_Wq, L0_attn_Wk, L0_attn_Wv, L0_attn_Wg, L0_attn_gk_w1, L0_attn_gk_w2, L0_attn_gk_b, L0_attn_Wo, L0_attn_rms_w), axis=-1)
    x = _layernorm(x + _L0_ffn_ref(x, L0_ffn_w1_w, L0_ffn_w1_s, L0_ffn_w2_w, L0_ffn_w2_s, L0_ffn_h1_w, L0_ffn_h1_s, L0_ffn_h2_w, L0_ffn_h2_s, L0_ffn_w3_w, L0_ffn_w3_s), axis=-1)
    return x

_drawn_inputs = setup_inputs


def setup_inputs(seed=0):
    import zlib

    import numpy as np

    out = dict(_drawn_inputs(seed))
    spreads = {'L0_attn_gk_b': (0.0, 0.8), 'L0_attn_rms_w': (1.0, 0.6)}
    factors = {'L0_attn_gk_w1': 64.0,
     'L0_attn_gk_w2': 61.075,
     'L0_ffn_w1_w': 8.0,
     'L0_ffn_w1_s': 8.0,
     'L0_ffn_w2_w': 8.0,
     'L0_ffn_w2_s': 8.0,
     'L0_ffn_h1_w': 8.0,
     'L0_ffn_h1_s': 8.0,
     'L0_ffn_h2_w': 8.0,
     'L0_ffn_h2_s': 8.0,
     'L0_ffn_w3_w': 8.0,
     'L0_ffn_w3_s': 8.0}
    for name, (base, spread) in spreads.items():
        noise = np.random.default_rng([zlib.crc32(name.encode()), seed]).standard_normal(out[name].shape)
        drawn = base * np.exp(spread * noise) if base else spread * noise
        out[name] = jnp.asarray(drawn.astype(out[name].dtype))
    for name, factor in factors.items():
        out[name] = (out[name] * factor).astype(out[name].dtype)
    return out
```

```python
import numpy as np
import concourse.bass as bass
from concourse import mybir
from contextlib import ExitStack

F32 = mybir.dt.float32
F32R = mybir.dt.float32r
I32 = mybir.dt.int32
ALU = mybir.AluOpType
ACT = mybir.ActivationFunctionType
AX = mybir.AxisListType.X

P = 128
B, T, D = 4, 1024, 256
H, HK, HV = 4, 64, 128
LR = 16
DV = H * HV
C = 128
NT = T // C
TOK = B * C
KC = D // P
HP = H // 2
G = HP * B
LEVELS = 7
HID = 1024
MC = HID // P
EPS = 1e-5
GATE_NORM = 16.0
NG = 15
N123 = 2 * KC * HID + MC * D
NH = MC * HID
LOOKS = 4
NCHECK = NT * LOOKS
CW = (N123 + 2 * NH) // NCHECK


def level_masks():
    m = np.zeros((P, LEVELS, 64), np.float32)
    for l in range(LEVELS):
        s = 1 << l
        for col in range(64):
            block = col // s
            m[2 * s * block:2 * s * block + s, l, col] = 1.0
    return m


def build(nc, x, xT, w_attn, w_o, gk1, gk2, gk_b, rms_w, w123, wh1, wh2, s_in, w3_s, consts, out):
    ctx = ExitStack()
    with ctx:
        def sem(name):
            return ctx.enter_context(nc.semaphore(name))

        def sb_in(scope):
            return lambda name, shape, dt=F32: scope.enter_context(nc.sbuf_tensor(name, shape, dt))

        sb = sb_in(ctx)
        ps = ctx.enter_context(nc.psum_tensor("ps", [P, 8, 512], F32))
        bank_g = [0, 1, 2]
        bank_s = [3, 4]
        bank_o = [5, 6]
        bank_x = 7

        x1 = sb("x1", [P, NT * B * D])

        def x1_tile(t):
            return x1[:, bass.ds(t * (B * D), B * D)]

        def x1_row(t, b):
            return x1[:, bass.ds(t * (B * D) + b * D, D)]

        w123r = sb("w123r", [P, 2 * KC * HID + MC * D], F32R)
        cst = sb("cst", [P, LEVELS * 64 + P + 2])
        w3s = sb("w3s", [P, D])
        scales = sb("scales", [P, 4, MC])
        small = sb("small", [P, 160])
        flag_i = sb("flag_i", [P, 1], I32)
        masks = cst[:, 0:LEVELS * 64].rearrange("p (l c) -> p l c", l=LEVELS)
        ident = cst[:, LEVELS * 64:LEVELS * 64 + P]
        select = cst[:, LEVELS * 64 + P:]
        stats = small[:, 0:24].rearrange("p (b s) -> p b s", b=B)
        mv = small[:, 24:32].rearrange("p (b s) -> p b s", b=B)
        rstd = small[:, 32:36]
        vare = small[:, 36:40]
        sdev = small[:, 40:44]
        ssum = small[:, 48:64]
        smean = small[:, 64:80]
        sroot = small[:, 80:96]
        rrms = small[:, 96:112]
        flag_p = small[:, 112:113]
        flag_f = small[:, 113:114]
        unequal = small[:, 120:120 + NCHECK]

        sa = ExitStack()
        a_ = sb_in(sa)
        wa_hi = a_("wa_hi", [P, KC, 6 * D], F32R)
        wa_lo = a_("wa_lo", [P, KC, 6 * D], F32R)
        xs = a_("xs", [P, KC, TOK])
        x_hi = a_("x_hi", [P, KC, TOK], F32R)
        x_lo = a_("x_lo", [P, KC, TOK], F32R)
        q = a_("q", [P, G, C])
        k = a_("k", [P, G, C])
        qs = a_("qs", [P, G, C])
        decay = a_("decay", [P, G, C])
        gl = a_("gl", [P, G, C])
        ex = a_("ex", [P, G, C])
        qk = a_("qk", [P, G, C])
        tot = a_("tot", [P, G, C])
        wo_hi = a_("wo_hi", [P, H, D], F32R)
        wo_lo = a_("wo_lo", [P, H, D], F32R)
        vg = a_("vg", [P, 2 * B * DV])
        v = vg[:, 0:B * DV].rearrange("p (b n) -> p b n", b=B)
        gate = vg[:, B * DV:].rearrange("p (b n) -> p b n", b=B)
        raw_attn = vg[:, 0:KC * 6 * D].rearrange("p (c n) -> p c n", c=KC)
        raw_o = vg[:, KC * 6 * D:].rearrange("p (h n) -> p h n", h=H)
        att = a_("att", [P, 2, G, C])
        kt = a_("kt", [P, G, C])
        state = a_("state", [P, G, 2, HV])
        og = a_("og", [P, B, DV])
        sq = a_("sq", [P, DV])
        ogt_hi = a_("ogt_hi", [P, H, P], F32R)
        ogt_lo = a_("ogt_lo", [P, H, P], F32R)
        xtok = a_("xtok", [P, B, D])
        y = a_("y", [P, B, D])
        gk1_sb = a_("gk1_sb", [P, KC, LR])
        gk2_sb = a_("gk2_sb", [LR, D])
        gkb_sb = a_("gkb_sb", [P, HP])
        rms = a_("rms", [P, HV])
        r_sb = a_("r_sb", [LR, TOK])
        stage = a_("stage", [P, 2, CW])
        rounded = a_("rounded", [P, CW], F32R)
        sa.close()
        tot_at = {l: sum(G * (C >> m) for m in range(1, l)) for l in range(1, LEVELS + 1)}

        def total(l):
            n = C >> l
            if l == 0:
                return decay[:, :, :]
            flat = tot[:, :, :].rearrange("p g c -> p (g c)")
            return flat[:, tot_at[l]:tot_at[l] + G * n].rearrange("p (g n) -> p g n", g=G)

        sbs = ExitStack()
        b_ = sb_in(sbs)
        wh1r = b_("wh1r", [P, MC, HID], F32R)
        wh2r = b_("wh2r", [P, MC, HID], F32R)
        ha_hi = b_("ha_hi", [P, MC, TOK], F32R)
        ha_lo = b_("ha_lo", [P, MC, TOK], F32R)
        hb_hi = b_("hb_hi", [P, MC, TOK], F32R)
        hb_lo = b_("hb_lo", [P, MC, TOK], F32R)
        x1t_hi = b_("x1t_hi", [P, KC, TOK], F32R)
        x1t_lo = b_("x1t_lo", [P, KC, TOK], F32R)
        xcur = b_("xcur", [P, B, D])
        sil = b_("sil", [P, TOK])
        hf = b_("hf", [P, 2, TOK])
        scaled = b_("scaled", [P, D])
        sbs.close()
        w1r = w123r[:, 0:KC * HID].rearrange("p (c n) -> p c n", c=KC)
        w2r = w123r[:, KC * HID:2 * KC * HID].rearrange("p (c n) -> p c n", c=KC)
        w3r = w123r[:, 2 * KC * HID:].rearrange("p (c n) -> p c n", c=MC)

        dw = nc.dram_tensor("dw", [P, N123 + 2 * NH], F32, kind="Internal").ap()

        consts_in = sem("consts_in")
        wraw_in = sem("wraw_in")
        copied = sem("copied")
        w123_in = sem("w123_in")
        wh1_in = sem("wh1_in")
        wh2_in = sem("wh2_in")
        stage_in = [sem("stage_in0"), sem("stage_in1")]
        rounded_done = sem("rounded_done")
        checked = sem("checked")
        flag_done = sem("flag_done")
        zeroed = sem("zeroed")
        w_split = sem("w_split")
        x_in = sem("x_in")
        xtok_in = sem("xtok_in")
        x_split = sem("x_split")
        g_done = sem("g_done")
        g_out = sem("g_out")
        ln_g = sem("ln_g")
        neg_g = sem("neg_g")
        act_chain = sem("act_chain")
        dve_chain = sem("dve_chain")
        decay_ready = sem("decay_ready")
        q_ready = sem("q_ready")
        k_ready = sem("k_ready")
        tot_ready = sem("tot_ready")
        qk_ready = sem("qk_ready")
        lev_done = sem("lev_done")
        lev_out = sem("lev_out")
        diag_done = sem("diag_done")
        diag_out = sem("diag_out")
        kt_done = sem("kt_done")
        kt_out = sem("kt_out")
        o_done = sem("o_done")
        sq_done = sem("sq_done")
        o_out = sem("o_out")
        gw_ready = sem("gw_ready")
        st_done = sem("st_done")
        st_out = sem("st_out")
        rms_in = sem("rms_in")
        rms_root = sem("rms_root")
        og_ready = sem("og_ready")
        ogt_done = sem("ogt_done")
        ogt_hi_out = sem("ogt_hi_out")
        ogt_lo_out = sem("ogt_lo_out")
        wo_done = sem("wo_done")
        y_out = sem("y_out")
        ln_in = sem("ln_in")
        ln_root = sem("ln_root")
        x1_done = sem("x1_done")
        xh_done = sem("xh_done")
        rrms_done = sem("rrms_done")
        st_stats = sem("st_stats")
        st_aggr = sem("st_aggr")
        rstd_done = sem("rstd_done")
        flag_local = sem("flag_local")
        flag_all = sem("flag_all")
        xcur_ready = sem("xcur_ready")
        tp_done = sem("tp_done")
        tp_hi = sem("tp_hi")
        tp_lo = sem("tp_lo")
        f1_done = sem("f1_done")
        sil_done = sem("sil_done")
        ha_ready = sem("ha_ready")
        f23_done = sem("f23_done")
        gelu_done = sem("gelu_done")
        hi_ready = sem("hi_ready")
        lo_ready = sem("lo_ready")
        f4_done = sem("f4_done")
        f4_out = sem("f4_out")
        ln2_in = sem("ln2_in")
        ln2_root = sem("ln2_root")
        y2_ready = sem("y2_ready")
        res2 = sem("res2")
        stored = sem("stored")

        block = ctx.enter_context(nc.Block())
        passed = {nc.vector.engine: sem("passed_dve"), nc.gpsimd.engine: sem("passed_pool")}

        def wait_alone(eng, semaphore, value):
            eng.wait_ge(semaphore, value)
            eng.sem_inc(passed[eng.engine], 1)

        def g_vg(t, j):
            return t * NG + (7 + j)

        def g_next(t, j):
            return t * NG + (15 + j)

        @block.sync
        def _(sp):
            sp.dma_start(raw_attn, w_attn).then_inc(wraw_in, 16)
            sp.dma_start(raw_o, w_o).then_inc(wraw_in, 16)
            sp.dma_start(xs[:], xT[0]).then_inc(x_in, 16)
            sp.dma_start(cst[:], consts).then_inc(consts_in, 16)
            sp.dma_start(gk1_sb[:], gk1).then_inc(consts_in, 16)
            sp.dma_start(gk2_sb[:], gk2).then_inc(consts_in, 16)
            sp.dma_start(gkb_sb[:], gk_b).then_inc(consts_in, 16)
            sp.dma_start(rms[:], rms_w.partition_broadcast(P)).then_inc(consts_in, 16)
            sp.dma_start(w3s[:], w3_s.partition_broadcast(P)).then_inc(consts_in, 16)
            sp.dma_start(scales[:], s_in).then_inc(consts_in, 16)
            sp.dma_start(dw[:, 0:N123], w123).then_inc(copied, 16)
            sp.dma_start(dw[:, N123:N123 + NH], wh1).then_inc(copied, 16)
            sp.dma_start(dw[:, N123 + NH:], wh2).then_inc(copied, 16)
            sp.wait_ge(copied, 48)
            sp.dma_start(w123r[:].bitcast(F32), dw[:, 0:N123]).then_inc(w123_in, 16)

            def stage_piece(t, i, free=True):
                if free:
                    sp.wait_ge(checked, t * LOOKS + i - 1)
                sp.dma_start(stage[:, i % 2, :], dw[:, bass.ds(t * LOOKS * CW + i * CW, CW)]).then_inc(stage_in[i % 2], 16)

            def tile_loads(t, more_x=True, first=False):
                stage_piece(t, 0, free=not first)
                stage_piece(t, 1, free=not first)
                if more_x:
                    sp.wait_ge(x_split, t + 1)
                    sp.dma_start(xs[:], xT[bass.ds(t + 1, 1)].rearrange("o p c n -> (o p) c n")).then_inc(x_in, 16)
                if not first:
                    sp.wait_ge(y_out, t * B)
                sp.dma_start(xtok[:], x[:, bass.ds(t * C, C), :].rearrange("b p d -> p b d")).then_inc(xtok_in, 16)
                stage_piece(t, 2)
                stage_piece(t, 3)

            tile_loads(0, first=True)
            with sp.Fori(1, NT - 1) as t:
                tile_loads(t)
            tile_loads(NT - 1, more_x=False)
            sp.wait_ge(g_done, g_vg(NT - 1, 8))
            sp.wait_ge(flag_done, 1)
            sp.dma_start(wh1r[:].bitcast(F32), dw[:, N123:N123 + NH].rearrange("p (c n) -> p c n", c=MC)).then_inc(wh1_in, 16)
            sp.wait_ge(st_done, NT * B)
            sp.wait_ge(st_out, NT * B)
            sp.dma_start(wh2r[:].bitcast(F32), dw[:, N123 + NH:].rearrange("p (c n) -> p c n", c=MC)).then_inc(wh2_in, 16)
            with sp.Fori(0, NT) as t:
                sp.wait_ge(y2_ready, t + 1)
                sp.dma_start(out[:, bass.ds(t * C, C), :].rearrange("b p d -> p b d"),
                             x1_tile(t).rearrange("p (b d) -> p b d", b=B)).then_inc(stored, 16)
            sp.wait_ge(stored, 16 * NT)

        @block.tensor
        def _(pe):
            def split_product(dst, pairs):
                n = 3 * len(pairs)
                i = 0
                for w_hi, w_lo, x_h, x_l in pairs:
                    for a, b in ((w_hi, x_h), (w_hi, x_l), (w_lo, x_h)):
                        last = nc.tensor.matmul(dst, a, b, start=i == 0, stop=i == n - 1)
                        i += 1
                return last

            def feature_group(n, j, t_is_first=False):
                if not (t_is_first and j < 3):
                    pe.wait_ge(g_out, n - 2)
                bank = bank_g[j % 3]
                if j == 0:
                    for c in range(KC):
                        last = nc.tensor.matmul(ps[0:LR, bank, :], gk1_sb[:, c, :],
                                                x_hi[:, c, :].bitcast(F32), start=c == 0, stop=False)
                    for c in range(KC):
                        last = nc.tensor.matmul(ps[0:LR, bank, :], gk1_sb[:, c, :],
                                                x_lo[:, c, :].bitcast(F32), start=False, stop=c == KC - 1)
                elif j < 3:
                    pe.wait_ge(g_out, n - j + 1)
                    m = j - 1
                    last = nc.tensor.matmul(ps[:, bank, :], gk2_sb[:, m * P:(m + 1) * P], r_sb[:],
                                            start=True, stop=True)
                else:
                    off = (j - 3) * P
                    last = split_product(ps[:, bank, :], [
                        (wa_hi[:, c, off:off + P], wa_lo[:, c, off:off + P], x_hi[:, c, :], x_lo[:, c, :])
                        for c in range(KC)])
                last.then_inc(g_done, 1)

            def token_group(t, j):
                pe.wait_ge(g_out, g_vg(t, j) - 2)
                b = j % B
                off = 2 * D if j < B else 4 * D
                last = split_product(ps[:, bank_g[(7 + j) % 3], :], [
                    (x_hi[:, c, b * C:(b + 1) * C], x_lo[:, c, b * C:(b + 1) * C],
                     wa_hi[:, c, off:off + DV], wa_lo[:, c, off:off + DV]) for c in range(KC)])
                last.then_inc(g_done, 1)

            def level(t, l):
                s = 1 << l
                pe.wait_ge(q_ready, t * 8 + (l + 1))
                if l == 0:
                    pe.wait_ge(g_out, t * NG + 7)
                else:
                    pe.wait_ge(k_ready, t * LEVELS + l)
                    pe.wait_ge(lev_out, t * LEVELS + l)
                for g in range(G):
                    for par in range(2):
                        rows = slice(par * HK, (par + 1) * HK)
                        right = qs[rows, g, :].rearrange("p (n s) -> p n s", s=2 * s)[:, :, s:2 * s]
                        last = nc.tensor.matmul(
                            ps[:, bank_s[par], g * 64:(g + 1) * 64], k[rows, g, :], right,
                            start=True, stop=True)
                last.then_inc(lev_done, 1)

            def diag(t):
                pe.wait_ge(qk_ready, t + 1)
                for g in range(G):
                    last = nc.tensor.matmul(ps[:, bank_x, 2 * g:2 * g + 2], qk[:, g, :], select,
                                            start=True, stop=True)
                last.then_inc(diag_done, 1)

            def transpose_o(t, b):
                if b == 0:
                    pe.wait_ge(diag_out, t + 2)
                else:
                    pe.wait_ge(ogt_lo_out, t * B + b)
                pe.wait_ge(og_ready, t * B + b + 1)
                for h in range(H):
                    last = nc.tensor.transpose(ps[:, bank_x, h * P:(h + 1) * P],
                                               og[:, b, h * P:(h + 1) * P], ident)
                last.then_inc(ogt_done, 1)

            def project_o(t, b):
                pe.wait_ge(ogt_lo_out, t * B + b + 1)
                if b >= 2:
                    pe.wait_ge(y_out, t * B + b - 1)
                split_product(ps[:, bank_o[b % 2], 0:D], [
                    (ogt_hi[:, h, :], ogt_lo[:, h, :], wo_hi[:, h, :], wo_lo[:, h, :])
                    for h in range(H)]).then_inc(wo_done, 1)

            def transpose_k(t):
                pe.wait_ge(lev_out, t * LEVELS + LEVELS)
                pe.wait_ge(k_ready, t * LEVELS + LEVELS)
                for hp in range(HP):
                    for b in range(B):
                        g = hp * B + b
                        last = nc.tensor.transpose(ps[:, bank_s[hp], b * P:(b + 1) * P], k[:, g, :], ident)
                    last.then_inc(kt_done, 1)

            def attend(t, b, first):
                if b == 0:
                    pe.wait_ge(q_ready, t * 8 + 8)
                    pe.wait_ge(g_out, g_vg(t, 3) + 1)
                    pe.wait_ge(diag_out, t + 1)
                    if first:
                        pe.wait_ge(zeroed, 2)
                    else:
                        pe.wait_ge(y_out, t * B)
                        pe.wait_ge(st_out, t * B)
                if b >= 2:
                    pe.wait_ge(o_out, t * B + b - 1)
                for hp in range(HP):
                    g = hp * B + b
                    dst = ps[:, bank_o[b % 2], hp * 2 * HV:(hp + 1) * 2 * HV]
                    nc.tensor.matmul(dst, qs[:, g, :], state[:, g, :, :], start=True, stop=True)
                    for par in range(2):
                        h = 2 * hp + par
                        last = nc.tensor.matmul(dst[:, par * HV:(par + 1) * HV], att[:, par, g, :],
                                                v[:, b, h * HV:(h + 1) * HV], start=False, stop=True,
                                                skip_group_check=True)
                last.then_inc(o_done, 1)

            def new_state(t, b):
                pe.wait_ge(kt_out, t * HP + HP)
                if b >= 2:
                    pe.wait_ge(st_out, t * B + b - 1)
                for hp in range(HP):
                    g = hp * B + b
                    last = nc.tensor.matmul(ps[:, bank_s[b % 2], hp * 2 * HV:(hp + 1) * 2 * HV], kt[:, g, :],
                                            v[:, b, hp * 2 * HV:(hp + 1) * 2 * HV], start=True, stop=True)
                last.then_inc(st_done, 1)

            def tile(t, first=False, last=False):
                level(t, 0)
                diag(t)
                token_group(t, 0)
                level(t, 1)
                if not first:
                    transpose_o(t - 1, 0)
                token_group(t, 1)
                for b in range(3):
                    level(t, 2 + b)
                    if not first:
                        project_o(t - 1, b)
                        transpose_o(t - 1, b + 1)
                    token_group(t, 2 + b)
                level(t, 5)
                if not first:
                    project_o(t - 1, 3)
                token_group(t, 5)
                level(t, 6)
                token_group(t, 6)
                token_group(t, 7)
                transpose_k(t)
                nxt = (lambda j: None) if last else (lambda j: feature_group(g_next(t, j), j))
                attend(t, 0, first)
                if not last:
                    pe.wait_ge(x_split, t + 2)
                nxt(0)
                new_state(t, 0)
                attend(t, 1, first)
                nxt(1)
                nxt(2)
                new_state(t, 1)
                nxt(3)
                attend(t, 2, first)
                nxt(4)
                new_state(t, 2)
                attend(t, 3, first)
                nxt(5)
                nxt(6)
                new_state(t, 3)

            pe.wait_ge(consts_in, 7 * 16)
            pe.wait_ge(x_split, 1)
            feature_group(0, 0, True)
            feature_group(1, 1, True)
            feature_group(2, 2, True)
            pe.wait_ge(w_split, 1)
            for j in range(3, 7):
                feature_group(j, j)
            tile(0, first=True)
            with pe.Fori(1, NT - 1) as t:
                tile(t)
            tile(NT - 1, last=True)
            pe.wait_ge(q_ready, 8 * NT)
            for b in range(B):
                pe.wait_ge(og_ready, (NT - 1) * B + b + 1)
                if b:
                    pe.wait_ge(ogt_lo_out, (NT - 1) * B + b)
                for h in range(H):
                    last = nc.tensor.transpose(ps[:, bank_x, h * P:(h + 1) * P],
                                               og[:, b, h * P:(h + 1) * P], ident)
                last.then_inc(ogt_done, 1)
                project_o(NT - 1, b)

            def ffn(exact):
                as_is = (lambda a: a) if exact else (lambda a: a.bitcast(F32))

                def product(dst, w, h_hi, h_lo, m, ready):
                    n = w.shape[1]
                    for c in range(n):
                        ready(c)
                        for half in (h_hi, h_lo):
                            last = nc.tensor.matmul(
                                dst, as_is(w[:, c, m * P:(m + 1) * P]), as_is(half[:, c, :]),
                                start=c == 0 and half is h_hi, stop=c == n - 1 and half is h_lo)
                    return last

                def transpose_x1(t):
                    pe.wait_ge(xcur_ready, t + 1)
                    for c in range(KC):
                        for b in range(B):
                            last = nc.tensor.transpose(ps[:, 6 + c, b * C:(b + 1) * C],
                                                       xcur[:, b, c * P:(c + 1) * P], ident)
                        last.then_inc(tp_done, 1)

                def ffn_tile(t, first=False, last=False):
                    for m in range(MC):
                        if m < 2:
                            if not first:
                                pe.wait_ge(gelu_done, t * 2 * MC - 2 + 2 * m)
                        else:
                            pe.wait_ge(ha_ready, t * MC + m - 1)
                        def ready(c):
                            if m == 0:
                                pe.wait_ge(tp_lo, t * KC + c + 1)
                        product(ps[:, 2 * (m % 2), :], w1r, x1t_hi, x1t_lo, m, ready)
                        product(ps[:, 2 * (m % 2) + 1, :], w2r, x1t_hi, x1t_lo, m,
                                lambda c: None).then_inc(f1_done, 1)
                    if first:
                        pe.wait_ge(wh1_in, 16)
                    for m in range(MC):
                        if m < 4:
                            pe.wait_ge(ha_ready, t * MC + MC - 1 + m // 2)
                        else:
                            pe.wait_ge(gelu_done, t * 2 * MC + m - 3)
                        def ready(c):
                            if m == 0:
                                pe.wait_ge(lo_ready, t * 3 * MC + c + 1)
                        product(ps[:, m % 4, :], wh1r, ha_hi, ha_lo, m, ready).then_inc(f23_done, 1)
                    if first:
                        pe.wait_ge(wh2_in, 16)
                    if not last:
                        transpose_x1(t + 1)
                    for m in range(MC):
                        pe.wait_ge(gelu_done, t * 2 * MC + MC + m - 3)
                        def ready(c):
                            if m == 0:
                                pe.wait_ge(lo_ready, t * 3 * MC + MC + c + 1)
                        product(ps[:, m % 4, :], wh2r, hb_hi, hb_lo, m, ready).then_inc(f23_done, 1)
                    for b in range(B):
                        if not (first and b < 2):
                            pe.wait_ge(f4_out, t * B + b - 1)
                        i = 0
                        for c in range(MC):
                            if b == 0:
                                pe.wait_ge(lo_ready, t * 3 * MC + 2 * MC + c + 1)
                            for half in (ha_hi, ha_lo):
                                mm = nc.tensor.matmul(
                                    ps[:, 4 + b % 2, 0:D], as_is(half[:, c, b * C:(b + 1) * C]),
                                    as_is(w3r[:, c, :]), start=i == 0, stop=i == 2 * MC - 1)
                                i += 1
                        mm.then_inc(f4_done, 1)

                transpose_x1(0)
                ffn_tile(0, first=True)
                with pe.Fori(1, NT - 1) as t:
                    ffn_tile(t)
                ffn_tile(NT - 1, last=True)

            pe.wait_ge(x1_done, NT)
            pe.wait_ge(w123_in, 16)
            pe.wait_ge(flag_done, 1)
            odd_weights = pe.value_load(flag_i[0:1, 0:1], min_val=0, max_val=1)
            with pe.If(odd_weights == 0):
                ffn(True)
            with pe.Else():
                ffn(False)

        @block.scalar
        def _(act):
            chain = [0]

            def evacuate(n, j, dst, func, **kw):
                act.wait_ge(g_done, n + 1)
                nc.scalar.activation(dst, ps[0:dst.shape[0], bank_g[j % 3], :], func, **kw).then_inc(g_out, 1)

            def half(hp):
                return slice(hp * B, (hp + 1) * B)

            def feature_out(n, j):
                if j == 0:
                    evacuate(n, j, r_sb[:], ACT.Copy)
                elif j < 3:
                    evacuate(n, j, gl[:, half(j - 1), :].rearrange("p b c -> p (b c)"), ACT.Identity,
                             bias=gkb_sb[:, j - 1:j])
                elif j < 5:
                    evacuate(n, j, q[:, half(j - 3), :].rearrange("p b c -> p (b c)"), ACT.Copy,
                             scale=HK ** -0.5)
                else:
                    evacuate(n, j, k[:, half(j - 5), :].rearrange("p b c -> p (b c)"), ACT.Copy)

            def softplus(t, n):
                act.wait_ge(g_out, n)
                nc.scalar.activation(ex[:], gl[:], ACT.Abs).then_inc(act_chain, 1)
                act.wait_ge(act_chain, t * 2 + 1)
                nc.scalar.activation(ex[:], ex[:], ACT.Exp, scale=-1.0).then_inc(act_chain, 1)
                act.wait_ge(act_chain, t * 2 + 2)
                nc.scalar.activation(ex[:], ex[:], ACT.Ln, bias=1.0).then_inc(ln_g, 1)

            def decays(t):
                act.wait_ge(neg_g, t + 1)
                nc.scalar.activation(decay[:], ex[:], ACT.Exp, scale=1.0 / GATE_NORM).then_inc(decay_ready, 1)

            def hi_o(t, b):
                act.wait_ge(ogt_done, t * B + b + 1)
                nc.scalar.activation(ogt_hi[:].rearrange("p h c -> p (h c)"), ps[:, bank_x, :],
                                     ACT.Copy).then_inc(ogt_hi_out, 1)

            def v_out(t, b):
                evacuate(g_vg(t, b), 7 + b, v[:, b, :], ACT.Copy)

            def gate_out(t, b):
                evacuate(g_vg(t, 4 + b), 11 + b, gate[:, b, :], ACT.Silu)

            def square(t, b):
                act.wait_ge(o_done, t * B + b + 1)
                if b:
                    act.wait_ge(o_out, t * B + b)
                nc.scalar.activation(sq[:], ps[:, bank_o[b % 2], :], ACT.Square).then_inc(sq_done, 1)

            def tile(t, first=False, last=False):
                v_out(t, 0)
                if not first:
                    hi_o(t - 1, 0)
                for b in range(1, 4):
                    v_out(t, b)
                    if not first:
                        hi_o(t - 1, b)
                for b in range(4):
                    gate_out(t, b)
                if not first:
                    act.wait_ge(ln_in, t)
                    nc.scalar.activation(sdev, vare, ACT.Sqrt).then_inc(ln_root, 1)
                for hp in range(HP):
                    act.wait_ge(kt_done, t * HP + hp + 1)
                    nc.scalar.activation(kt[:, half(hp), :].rearrange("p b c -> p (b c)"),
                                         ps[:, bank_s[hp], :], ACT.Copy).then_inc(kt_out, 1)
                nxt = (lambda j: None) if last else (lambda j: feature_out(g_next(t, j), j))
                square(t, 0)
                nxt(0)
                square(t, 1)
                nxt(1)
                nxt(2)
                if not last:
                    softplus(t + 1, g_next(t, 3))
                nxt(3)
                square(t, 2)
                nxt(4)
                if not last:
                    decays(t + 1)
                square(t, 3)
                nxt(5)
                nxt(6)
                act.wait_ge(rms_in, t + 1)
                nc.scalar.activation(sroot, smean, ACT.Sqrt).then_inc(rms_root, 1)

            act.wait_ge(consts_in, 7 * 16)
            for j in range(3):
                feature_out(j, j)
            softplus(0, 3)
            for j in range(3, 7):
                feature_out(j, j)
            decays(0)
            tile(0, first=True)
            with act.Fori(1, NT - 1) as t:
                tile(t)
            tile(NT - 1, last=True)
            for b in range(B):
                hi_o(NT - 1, b)
            act.wait_ge(ln_in, NT)
            nc.scalar.activation(sdev, vare, ACT.Sqrt).then_inc(ln_root, 1)

            def x1_hi(t):
                for c in range(KC):
                    act.wait_ge(tp_done, t * KC + c + 1)
                    nc.scalar.activation(x1t_hi[:, c, :], ps[:, 6 + c, :], ACT.Copy).then_inc(tp_hi, 1)

            def gelu(t, layer, m):
                j = layer * MC + m
                act.wait_ge(f23_done, t * 2 * MC + (j - MC) + 1)
                act.wait_ge(lo_ready, t * 3 * MC + j - 1)
                nc.scalar.activation(hf[:, m % 2, :], ps[:, m % 4, :], ACT.Gelu,
                                     scale=scales[:, layer + 1, m:m + 1]).then_inc(gelu_done, 1)

            def ffn_tile(t, first=False, last=False):
                for m in range(MC):
                    act.wait_ge(f1_done, t * MC + m + 1)
                    if not (first and m == 0):
                        act.wait_ge(ha_ready, t * MC + m)
                    nc.scalar.activation(sil[:], ps[:, 2 * (m % 2), :], ACT.Silu,
                                         scale=scales[:, 0, m:m + 1]).then_inc(sil_done, 1)
                for m in range(MC):
                    gelu(t, 1, m)
                if not last:
                    x1_hi(t + 1)
                for m in range(MC):
                    gelu(t, 2, m)
                act.wait_ge(ln2_in, t + 1)
                nc.scalar.activation(sdev, vare, ACT.Sqrt).then_inc(ln2_root, 1)

            x1_hi(0)
            ffn_tile(0, first=True)
            with act.Fori(1, NT - 1) as t:
                ffn_tile(t)
            ffn_tile(NT - 1, last=True)

        @block.vector
        def _(dve):
            def split_x(t):
                dve.wait_ge(x_in, t * 16 + 16)
                nc.vector.tensor_copy(x_hi[:], xs[:]).then_inc(xh_done, 1)
                dve.wait_ge(xh_done, t + 1)
                nc.vector.tensor_tensor(x_lo[:], xs[:], x_hi[:].bitcast(F32), ALU.subtract).then_inc(x_split, 1)

            def start_q(t, n_q):
                dve.wait_ge(g_out, n_q)
                dve.wait_ge(decay_ready, t + 1)
                nc.vector.tensor_tensor(qs[:], q[:], decay[:], ALU.mult).then_inc(q_ready, 1)

            def level(t, l, first=False):
                s = 1 << l
                dve.wait_ge(lev_done, t * LEVELS + (l + 1))
                dve.wait_ge(q_ready, t * 8 + (l + 1))
                if l or not first:
                    dve.wait_ge(lev_out, t * LEVELS + l)
                if l == 1:
                    dve.wait_ge(diag_out, t + 1)
                if l:
                    dve.wait_ge(tot_ready, t * LEVELS + l)
                left = total(l).rearrange("p g (n two) -> p g n two", two=2)[:, :, :, 0:1]
                n = C // (2 * s)
                right = qs[:].rearrange("p g (n s) -> p g n s", s=2 * s)[:, :, :, s:2 * s]
                nc.vector.tensor_tensor(right, right, left.to_broadcast([P, G, n, s]),
                                        ALU.mult).then_inc(q_ready, 1)
                for par in range(2):
                    dst = att[:, par, :, :].rearrange("p g (n s) -> p g n s", s=2 * s)[:, :, :, s:2 * s]
                    src = ps[:, bank_s[par], :].rearrange("p (g n s) -> p g n s", g=G, s=s)
                    msk = masks[:, l, :].bitcast(I32).rearrange("p (o n s) -> p o n s", o=1, s=s)
                    op = nc.vector.copy_predicated(dst, msk.to_broadcast([P, G, n, s]), src)
                op.then_inc(lev_out, 1)

            def diagonal(t):
                dve.wait_ge(lev_out, t * LEVELS + 1)
                wait_alone(dve, diag_done, t + 1)
                for par in range(2):
                    src = ps[:, bank_x, 0:2 * G].rearrange("p (g r o) -> p r g o", r=2, o=1)[:, par]
                    msk = ident.bitcast(I32).rearrange("p (o c) -> p o c", o=1)
                    op = nc.vector.copy_predicated(att[:, par, :, :], msk.to_broadcast([P, G, C]),
                                                   src.to_broadcast([P, G, C]))
                op.then_inc(diag_out, 1)

            def normed_heads(t):
                dve.wait_ge(rms_root, t + 1)
                nc.vector.reciprocal(rrms, sroot).then_inc(rrms_done, 1)
                dve.wait_ge(rrms_done, t + 1)
                for b in range(B):
                    o_h = og[:, b, :].rearrange("p (h n) -> p h n", h=H)
                    sc = rrms[:, b * H:(b + 1) * H].rearrange("p (h o) -> p h o", o=1)
                    nc.vector.tensor_tensor(o_h, o_h, sc.to_broadcast([P, H, HV]), ALU.mult).then_inc(og_ready, 1)

            def lo_o(t, b):
                dve.wait_ge(ogt_hi_out, t * B + b + 1)
                nc.vector.tensor_tensor(ogt_lo[:].rearrange("p h c -> p (h c)"), ps[:, bank_x, :],
                                        ogt_hi[:].bitcast(F32).rearrange("p h c -> p (h c)"),
                                        ALU.subtract).then_inc(ogt_lo_out, 1)

            def residual(t, b):
                if b == 0:
                    dve.wait_ge(xtok_in, t * 16 + 16)
                dve.wait_ge(wo_done, t * B + b + 1)
                nc.vector.tensor_tensor(y[:, b, :], ps[:, bank_o[b % 2], 0:D], xtok[:, b, :],
                                        ALU.add).then_inc(y_out, 1)
                dve.wait_ge(y_out, t * B + b + 1)
                nc.vector.bn_stats(stats[:, b, :], y[:, b, :]).then_inc(st_stats, 1)
                wait_alone(dve, st_stats, t * B + b + 1)
                nc.vector.bn_aggr(mv[:, b, :], stats[:, b, :]).then_inc(st_aggr, 1)

            def var_eps(n_aggr, done):
                dve.wait_ge(st_aggr, n_aggr)
                nc.vector.tensor_scalar(vare, mv[:, :, 1:2].rearrange("p b o -> p (b o)"), EPS, None,
                                        ALU.add).then_inc(done, 1)

            def norm_rows(src, dst, n_root, root, last_sem, n_rstd):
                dve.wait_ge(root, n_root)
                nc.vector.reciprocal(rstd, sdev).then_inc(rstd_done, 1)
                dve.wait_ge(rstd_done, n_rstd)
                for b in range(B):
                    op = nc.vector.tensor_scalar(dst(b), src(b), mv[:, b, 0:1], rstd[:, b:b + 1],
                                                 ALU.subtract, ALU.mult)
                op.then_inc(last_sem, 1)

            def finish_x1(t):
                norm_rows(lambda b: y[:, b, :], lambda b: x1_row(t, b), t + 1, ln_root, x1_done, t + 1)

            def neg_gate(t):
                dve.wait_ge(ln_g, t + 1)
                nc.vector.scalar_tensor_tensor(ex[:], gl[:], 0.0, ex[:], ALU.min, ALU.subtract).then_inc(neg_g, 1)

            def heads_out(t, b):
                dve.wait_ge(gw_ready, t * B + b + 1)
                dve.wait_ge(sq_done, t * B + b + 1)
                nc.vector.tensor_tensor(og[:, b, :], ps[:, bank_o[b % 2], :], gate[:, b, :], ALU.mult)
                nc.vector.tensor_reduce(ssum[:, b * H:(b + 1) * H], sq[:].rearrange("p (h n) -> p h n", h=H),
                                        AX, ALU.add).then_inc(o_out, 1)

            def state_out(t, b):
                dve.wait_ge(st_done, t * B + b + 1)
                if b == 0:
                    dve.wait_ge(tot_ready, t * LEVELS + LEVELS)
                for hp in range(HP):
                    g = hp * B + b
                    for par in range(2):
                        rows = slice(par * HK, (par + 1) * HK)
                        s_old = state[rows, g, par, :]
                        add = ps[rows, bank_s[b % 2], (2 * hp + par) * HV:(2 * hp + par + 1) * HV]
                        op = nc.vector.scalar_tensor_tensor(s_old, s_old, total(LEVELS)[rows, g, :], add,
                                                            ALU.mult, ALU.add)
                op.then_inc(st_out, 1)

            def look(t, i):
                dve.wait_ge(rounded_done, t * LOOKS + i + 1)
                nc.vector.scalar_tensor_tensor(rounded[:].bitcast(F32), stage[:, i % 2, :], 1.0,
                                               rounded[:].bitcast(F32), ALU.mult, ALU.not_equal,
                                               accum_out=unequal[:, bass.ds(t * LOOKS + i, 1)]).then_inc(checked, 1)

            def tile(t, first=False, last=False):
                start_q(t, t * NG + 5)
                level(t, 0, first)
                if not first:
                    normed_heads(t - 1)
                diagonal(t)
                level(t, 1)
                if not first:
                    lo_o(t - 1, 0)
                for b in range(3):
                    level(t, 2 + b)
                    if not first:
                        residual(t - 1, b)
                        lo_o(t - 1, b + 1)
                level(t, 5)
                look(t, 0)
                if not first:
                    residual(t - 1, 3)
                    var_eps(t * B, ln_in)
                level(t, 6)
                if not last:
                    dve.wait_ge(g_done, g_vg(t, 8))
                    split_x(t + 1)
                if not first:
                    finish_x1(t - 1)
                heads_out(t, 0)
                state_out(t, 0)
                look(t, 1)
                heads_out(t, 1)
                state_out(t, 1)
                if not last:
                    neg_gate(t + 1)
                look(t, 2)
                heads_out(t, 2)
                state_out(t, 2)
                look(t, 3)
                heads_out(t, 3)
                state_out(t, 3)
                dve.wait_ge(o_out, t * B + B)
                nc.vector.tensor_scalar(smean, ssum, 1.0 / HV, EPS, ALU.mult, ALU.add).then_inc(rms_in, 1)

            split_x(0)
            dve.wait_ge(wraw_in, 32)
            nc.vector.tensor_copy(wa_hi[:], raw_attn).then_inc(dve_chain, 1)
            nc.vector.tensor_copy(wo_hi[:], raw_o).then_inc(dve_chain, 1)
            dve.wait_ge(dve_chain, 2)
            nc.vector.tensor_tensor(wa_lo[:], raw_attn, wa_hi[:].bitcast(F32), ALU.subtract)
            nc.vector.tensor_tensor(wo_lo[:], raw_o, wo_hi[:].bitcast(F32), ALU.subtract).then_inc(w_split, 1)
            neg_gate(0)
            dve.wait_ge(zeroed, 1)
            tile(0, first=True)
            with dve.Fori(1, NT - 1) as t:
                tile(t)
            tile(NT - 1, last=True)
            normed_heads(NT - 1)
            for b in range(B):
                lo_o(NT - 1, b)
                residual(NT - 1, b)
            var_eps(NT * B, ln_in)
            dve.wait_ge(checked, NCHECK)
            nc.vector.tensor_reduce(flag_p, unequal, AX, ALU.max).then_inc(flag_local, 1)
            dve.wait_ge(flag_all, 1)
            nc.vector.tensor_scalar(flag_i[:], flag_f, 0.0, None, ALU.is_gt).then_inc(flag_done, 1)
            finish_x1(NT - 1)

            def x1_lo(t):
                for c in range(KC):
                    dve.wait_ge(tp_hi, t * KC + c + 1)
                    nc.vector.tensor_tensor(x1t_lo[:, c, :], ps[:, 6 + c, :], x1t_hi[:, c, :].bitcast(F32),
                                            ALU.subtract).then_inc(tp_lo, 1)

            def lo_part(t, layer, m):
                dst = (ha_lo, hb_lo, ha_lo)[layer]
                hi = (ha_hi, hb_hi, ha_hi)[layer]
                dve.wait_ge(hi_ready, t * 3 * MC + layer * MC + m + 1)
                nc.vector.tensor_tensor(dst[:, m, :], hf[:, m % 2, :], hi[:, m, :].bitcast(F32),
                                        ALU.subtract).then_inc(lo_ready, 1)

            def ffn_tile(t, first=False, last=False):
                for m in range(MC):
                    dve.wait_ge(sil_done, t * MC + m + 1)
                    if m >= 2:
                        dve.wait_ge(lo_ready, t * 3 * MC + m - 1)
                    elif not first:
                        dve.wait_ge(y2_ready, t)
                    nc.vector.scalar_tensor_tensor(hf[:, m % 2, :], ps[:, 2 * (m % 2) + 1, :],
                                                   scales[:, 1, m:m + 1], sil[:], ALU.mult,
                                                   ALU.mult).then_inc(ha_ready, 1)
                    if m:
                        lo_part(t, 0, m - 1)
                lo_part(t, 0, MC - 1)
                for m in range(MC):
                    lo_part(t, 1, m)
                if not last:
                    x1_lo(t + 1)
                for m in range(MC):
                    lo_part(t, 2, m)
                y2 = hf[:].rearrange("p a (c d) -> p (a c) d", d=D)
                for b in range(B):
                    dve.wait_ge(f4_done, t * B + b + 1)
                    if b == 0:
                        dve.wait_ge(lo_ready, t * 3 * MC + 3 * MC)
                        if not first:
                            dve.wait_ge(res2, t * B)
                    else:
                        dve.wait_ge(res2, t * B + b)
                    nc.vector.tensor_tensor(scaled[:], ps[:, 4 + b % 2, 0:D], w3s[:], ALU.mult).then_inc(f4_out, 1)
                    dve.wait_ge(f4_out, t * B + b + 1)
                    nc.vector.tensor_tensor(y2[:, b, :], scaled[:], x1_row(t, b), ALU.add).then_inc(res2, 1)
                    dve.wait_ge(res2, t * B + b + 1)
                    nc.vector.bn_stats(stats[:, b, :], y2[:, b, :]).then_inc(st_stats, 1)
                    wait_alone(dve, st_stats, t * B + (NT * B + b + 1))
                    nc.vector.bn_aggr(mv[:, b, :], stats[:, b, :]).then_inc(st_aggr, 1)
                var_eps(t * B + (NT * B + B), ln2_in)
                norm_rows(lambda b: y2[:, b, :], lambda b: x1_row(t, b), t + 1, ln2_root, y2_ready, t + (NT + 1))

            x1_lo(0)
            ffn_tile(0, first=True)
            with dve.Fori(1, NT - 1) as t:
                ffn_tile(t)
            ffn_tile(NT - 1, last=True)

        @block.gpsimd
        def _(pool):
            nc.gpsimd.memset(att[:], 0.0).then_inc(zeroed, 1)
            nc.gpsimd.memset(state[:], 0.0).then_inc(zeroed, 1)
            pool.wait_ge(consts_in, 7 * 16)

            def totals(t, l):
                if l == 1:
                    pool.wait_ge(decay_ready, t + 1)
                else:
                    pool.wait_ge(tot_ready, t * LEVELS + (l - 1))
                pairs = total(l - 1).rearrange("p g (n two) -> p g n two", two=2)
                dst = total(l).rearrange("p g (n o) -> p g n o", o=1)
                nc.gpsimd.tensor_tensor(dst, pairs[:, :, :, 0:1], pairs[:, :, :, 1:2],
                                        ALU.mult).then_inc(tot_ready, 1)

            def level(t, l):
                s = 1 << l
                n = C // (2 * s)
                pool.wait_ge(lev_done, t * LEVELS + (l + 1))
                if l:
                    pool.wait_ge(k_ready, t * LEVELS + l)
                    pool.wait_ge(tot_ready, t * LEVELS + l)
                else:
                    pool.wait_ge(qk_ready, t + 1)
                right = total(l).rearrange("p g (n two) -> p g n two", two=2)[:, :, :, 1:2]
                left = k[:].rearrange("p g (n s) -> p g n s", s=2 * s)[:, :, :, 0:s]
                nc.gpsimd.tensor_tensor(left, left, right.to_broadcast([P, G, n, s]),
                                        ALU.mult).then_inc(k_ready, 1)

            def round_piece(t, i, free=True):
                wait_alone(pool, stage_in[i % 2], t * (LOOKS // 2 * 16) + (i // 2 + 1) * 16)
                if free:
                    wait_alone(pool, checked, t * LOOKS + i)
                nc.gpsimd.tensor_copy(rounded[:], stage[:, i % 2, :]).then_inc(rounded_done, 1)

            def tile(t, first=False):
                pool.wait_ge(g_out, t * NG + 7)
                nc.gpsimd.tensor_tensor(qk[:], q[:], k[:], ALU.mult).then_inc(qk_ready, 1)
                totals(t, 1)
                for l in range(LEVELS):
                    level(t, l)
                    if l + 2 <= LEVELS:
                        totals(t, l + 2)
                    if l == 4:
                        round_piece(t, 0, free=not first)
                for b in range(B):
                    pool.wait_ge(g_out, g_vg(t, 4 + b) + 1)
                    g_h = gate[:, b, :].rearrange("p (h n) -> p h n", h=H)
                    w_h = rms[:].rearrange("p (o n) -> p o n", o=1)
                    nc.gpsimd.tensor_tensor(g_h, g_h, w_h.to_broadcast([P, H, HV]), ALU.mult).then_inc(gw_ready, 1)
                for i in range(1, LOOKS):
                    round_piece(t, i)

            tile(0, first=True)
            with pool.Fori(1, NT) as t:
                tile(t)
            pool.wait_ge(flag_local, 1)
            nc.gpsimd.partition_all_reduce(flag_f, flag_p, P, bass.bass_isa.ReduceOp.max).then_inc(flag_all, 1)

            def copy_x1(t):
                nc.gpsimd.tensor_copy(xcur[:].rearrange("p b d -> p (b d)"), x1_tile(t)).then_inc(xcur_ready, 1)

            def hi_part(t, layer, m):
                if layer == 0:
                    wait_alone(pool, ha_ready, t * MC + m + 1)
                else:
                    wait_alone(pool, gelu_done, t * 2 * MC + (layer - 1) * MC + m + 1)
                dst = (ha_hi, hb_hi, ha_hi)[layer]
                nc.gpsimd.tensor_copy(dst[:, m, :], hf[:, m % 2, :]).then_inc(hi_ready, 1)

            def ffn_tile(t, last=False):
                for m in range(MC):
                    hi_part(t, 0, m)
                if not last:
                    wait_alone(pool, tp_done, t * KC + KC)
                    copy_x1(t + 1)
                for layer in (1, 2):
                    for m in range(MC):
                        hi_part(t, layer, m)

            wait_alone(pool, x1_done, NT)
            copy_x1(0)
            with pool.Fori(0, NT - 1) as t:
                ffn_tile(t)
            ffn_tile(NT - 1, last=True)


_OUTS = [((B, T, D), "float32")]


def kernel(**inputs):
    import concourse.bacc as _bacc
    from concourse.bass_utils import run_bass_kernel_spmd as _run

    a = {n: np.ascontiguousarray(v) for n, v in inputs.items()}

    def rows(w, chunks):
        return w.reshape(chunks, P, -1).transpose(1, 0, 2)

    x = a["L0_attn_x"]
    attn = rows(np.concatenate([a["L0_attn_Wq"], a["L0_attn_Wk"], a["L0_attn_Wv"], a["L0_attn_Wg"]], axis=1), KC)
    flat = lambda w: w.reshape(P, -1)
    consts = np.zeros((P, LEVELS * 64 + P + 2), np.float32)
    consts[:, :LEVELS * 64] = level_masks().reshape(P, -1)
    consts[:, LEVELS * 64:LEVELS * 64 + P] = np.eye(P, dtype=np.float32)
    consts[:HK, -2] = 1.0
    consts[HK:, -1] = 1.0
    sent = {
        "x": x,
        "xT": x.reshape(B, NT, C, KC, P).transpose(1, 4, 3, 0, 2).reshape(NT, P, KC, TOK),
        "w_attn": attn,
        "w_o": rows(a["L0_attn_Wo"], H),
        "gk1": rows(a["L0_attn_gk_w1"], KC),
        "gk2": a["L0_attn_gk_w2"],
        "gk_b": a["L0_attn_gk_b"].reshape(HP, P).T,
        "rms_w": a["L0_attn_rms_w"],
        "w123": np.concatenate([flat(rows(a["L0_ffn_w1_w"].T, KC)), flat(rows(a["L0_ffn_w2_w"].T, KC)),
                                flat(rows(a["L0_ffn_w3_w"].T, MC))], axis=1),
        "wh1": flat(rows(a["L0_ffn_h1_w"].T, MC)),
        "wh2": flat(rows(a["L0_ffn_h2_w"].T, MC)),
        "s_in": np.stack([a[f"L0_ffn_{n}_s"].reshape(MC, P).T for n in ("w1", "w2", "h1", "h2")], axis=1),
        "w3_s": a["L0_ffn_w3_s"],
        "consts": consts,
    }
    nc = _bacc.Bacc("TRN2", target_bir_lowering=False, num_devices=1)
    arrays, args = {}, []
    for name, v in sent.items():
        v = np.ascontiguousarray(v)
        arrays[f"in_{name}"] = v
        args.append(nc.dram_tensor(f"in_{name}", v.shape, mybir.dt.from_np(v.dtype), kind="ExternalInput").ap())
    for i, (shape, dtype) in enumerate(_OUTS):
        args.append(nc.dram_tensor(f"out_{i}", shape, mybir.dt.from_np(np.dtype(dtype)), kind="ExternalOutput").ap())
    build(nc, *args)
    r = _run(nc, [arrays], core_ids=[0])
    return r.results[0]["out_0"]
```

```python
import numpy as np
import concourse.bass as bass
from concourse import mybir
from contextlib import ExitStack

F32 = mybir.dt.float32
F32R = mybir.dt.float32r
I32 = mybir.dt.int32
ALU = mybir.AluOpType
ACT = mybir.ActivationFunctionType
AX = mybir.AxisListType.X

P = 128
B, T, D = 4, 1024, 256
H, HK, HV = 4, 64, 128
LR = 16
DV = H * HV
C = 128
NT = T // C
TOK = B * C
KC = D // P
HP = H // 2
G = HP * B
LEVELS = 7
HID = 1024
MC = HID // P
EPS = 1e-5
GATE_NORM = 16.0
NQ = HP * 8
NL = HP * 7
NG = 15
N123 = 2 * KC * HID + MC * D
NH = MC * HID
LOOKS = 4
NCHECK = NT * LOOKS
CW = (N123 + 2 * NH) // NCHECK


def level_masks():
    m = np.zeros((P, LEVELS, 64), np.float32)
    for l in range(LEVELS):
        s = 1 << l
        for col in range(64):
            block = col // s
            m[2 * s * block:2 * s * block + s, l, col] = 1.0
    return m


def build(nc, x, xT, w_attn, w_o, gk1, gk2, gk_b, rms_w, w123, wh1, wh2, s_in, w3_s, consts, level_mask, out):
    ctx = ExitStack()
    with ctx:
        def sem(name):
            return ctx.enter_context(nc.semaphore(name))

        def sb_in(scope):
            return lambda name, shape, dt=F32: scope.enter_context(nc.sbuf_tensor(name, shape, dt))

        sb = sb_in(ctx)
        ps = ctx.enter_context(nc.psum_tensor("ps", [P, 8, 512], F32))
        bank_g = [0, 1, 2]
        bank_s = [3, 4]
        bank_o = [5, 6]
        bank_x = 7

        x1 = sb("x1", [P, NT * B * D])

        def x1_tile(t):
            return x1[:, bass.ds(t * (B * D), B * D)]

        def x1_row(t, b):
            return x1[:, bass.ds(t * (B * D) + b * D, D)]

        w123r = sb("w123r", [P, 2 * KC * HID + MC * D], F32R)
        cst = sb("cst", [P, P + 2])
        w3s = sb("w3s", [P, D])
        scales = sb("scales", [P, 4, MC])
        small = sb("small", [P, 160])
        flag_i = sb("flag_i", [P, 1], I32)
        ident = cst[:, 0:P]
        select = cst[:, P:]
        stats = small[:, 0:24].rearrange("p (b s) -> p b s", b=B)
        mv = small[:, 24:32].rearrange("p (b s) -> p b s", b=B)
        rstd = small[:, 32:36]
        vare = small[:, 36:40]
        sdev = small[:, 40:44]
        ssum = small[:, 48:64]
        smean = small[:, 64:80]
        sroot = small[:, 80:96]
        rrms = small[:, 96:112]
        flag_p = small[:, 112:113]
        flag_f = small[:, 113:114]
        unequal = small[:, 120:120 + NCHECK]

        sa = ExitStack()
        a_ = sb_in(sa)
        wa_hi = a_("wa_hi", [P, KC, 6 * D], F32R)
        wa_lo = a_("wa_lo", [P, KC, 6 * D], F32R)
        xs = a_("xs", [P, KC, TOK])
        x_hi = a_("x_hi", [P, KC, TOK], F32R)
        x_lo = a_("x_lo", [P, KC, TOK], F32R)
        q = a_("q", [P, G, C])
        k = a_("k", [P, G, C])
        q2 = a_("q2", [P, G, 2, C])
        decay = a_("decay", [P, G, C])
        gl = a_("gl", [P, G, C])
        ex = a_("ex", [P, G, C])
        qk = ex
        tot = a_("tot", [P, G, C])
        wo_hi = a_("wo_hi", [P, H, D], F32R)
        wo_lo = a_("wo_lo", [P, H, D], F32R)
        vg = a_("vg", [P, 2 * B * DV])
        v = vg[:, 0:B * DV].rearrange("p (b n) -> p b n", b=B)
        gate = vg[:, B * DV:].rearrange("p (b n) -> p b n", b=B)
        raw_attn = vg[:, 0:KC * 6 * D].rearrange("p (c n) -> p c n", c=KC)
        raw_o = vg[:, KC * 6 * D:].rearrange("p (h n) -> p h n", h=H)
        att = a_("att", [P, G, 2, C])
        kt = a_("kt", [P, G, C])
        state = a_("state", [P, G, 2, HV])
        og = a_("og", [P, B, DV])
        sq = a_("sq", [P, DV])
        ogt_hi = a_("ogt_hi", [P, H, P], F32R)
        ogt_lo = a_("ogt_lo", [P, H, P], F32R)
        xtok = a_("xtok", [P, B, D])
        y = a_("y", [P, B, D])
        raw_gk1 = y[:, 0, 0:KC * LR].rearrange("p (c n) -> p c n", c=KC)
        gk1_hi = a_("gk1_hi", [P, KC, P], F32R)
        gk1_lo = a_("gk1_lo", [P, KC, P], F32R)
        gk2_sb = a_("gk2_sb", [LR, D])
        gkb_sb = a_("gkb_sb", [P, HP])
        rms = a_("rms", [P, HV])
        r_sb = y[0:LR, 2:4, :].rearrange("p b d -> p (b d)")
        masks = a_("masks", [P, LEVELS, 64])
        stage = a_("stage", [P, 2, CW])
        rounded = a_("rounded", [P, CW], F32R)
        sa.close()
        tot_at = {l: sum(G * (C >> m) for m in range(1, l)) for l in range(1, LEVELS + 1)}

        def total(l):
            n = C >> l
            if l == 0:
                return decay[:, :, :]
            flat = tot[:, :, :].rearrange("p g c -> p (g c)")
            return flat[:, tot_at[l]:tot_at[l] + G * n].rearrange("p (g n) -> p g n", g=G)

        sbs = ExitStack()
        b_ = sb_in(sbs)
        wh1r = b_("wh1r", [P, MC, HID], F32R)
        wh2r = b_("wh2r", [P, MC, HID], F32R)
        ha_hi = b_("ha_hi", [P, MC, TOK], F32R)
        ha_lo = b_("ha_lo", [P, MC, TOK], F32R)
        hb_hi = b_("hb_hi", [P, MC, TOK], F32R)
        hb_lo = b_("hb_lo", [P, MC, TOK], F32R)
        x1t_hi = b_("x1t_hi", [P, KC, TOK], F32R)
        x1t_lo = b_("x1t_lo", [P, KC, TOK], F32R)
        xcur = b_("xcur", [P, B, D])
        sil = b_("sil", [P, 2, TOK])
        hf = b_("hf", [P, 2, TOK])
        sbs.close()
        w1r = w123r[:, 0:KC * HID].rearrange("p (c n) -> p c n", c=KC)
        w2r = w123r[:, KC * HID:2 * KC * HID].rearrange("p (c n) -> p c n", c=KC)
        w3r = w123r[:, 2 * KC * HID:].rearrange("p (c n) -> p c n", c=MC)

        dw = nc.dram_tensor("dw", [P, N123 + 2 * NH], F32, kind="Internal").ap()

        consts_in = sem("consts_in")
        wraw_in = sem("wraw_in")
        copied = sem("copied")
        w123_in = sem("w123_in")
        wh1_in = sem("wh1_in")
        wh2_in = sem("wh2_in")
        stage_in = [sem("stage_in0"), sem("stage_in1")]
        rounded_done = sem("rounded_done")
        checked = sem("checked")
        flag_done = sem("flag_done")
        zeroed = sem("zeroed")
        gk1_split = sem("gk1_split")
        w_split = sem("w_split")
        x_in = sem("x_in")
        xtok_in = sem("xtok_in")
        x_split = sem("x_split")
        g_done = sem("g_done")
        g_out = sem("g_out")
        ln_g = sem("ln_g")
        neg_g = sem("neg_g")
        act_chain = sem("act_chain")
        dve_chain = sem("dve_chain")
        decay_ready = sem("decay_ready")
        q_ready = sem("q_ready")
        k_ready = sem("k_ready")
        tot_ready = sem("tot_ready")
        qk_ready = sem("qk_ready")
        lev_done = sem("lev_done")
        lev_out = sem("lev_out")
        diag_done = sem("diag_done")
        diag_out = sem("diag_out")
        kt_done = sem("kt_done")
        kt_out = sem("kt_out")
        o_done = sem("o_done")
        sq_done = sem("sq_done")
        o_out = sem("o_out")
        gw_ready = sem("gw_ready")
        st_done = sem("st_done")
        st_out = sem("st_out")
        rms_in = sem("rms_in")
        rms_root = sem("rms_root")
        og_ready = sem("og_ready")
        ogt_done = sem("ogt_done")
        ogt_hi_out = sem("ogt_hi_out")
        ogt_lo_out = sem("ogt_lo_out")
        wo_done = sem("wo_done")
        y_out = sem("y_out")
        ln_in = sem("ln_in")
        ln_root = sem("ln_root")
        x1_done = sem("x1_done")
        xh_done = sem("xh_done")
        rrms_done = sem("rrms_done")
        st_stats = sem("st_stats")
        st_aggr = sem("st_aggr")
        rstd_done = sem("rstd_done")
        flag_local = sem("flag_local")
        flag_all = sem("flag_all")
        xcur_ready = sem("xcur_ready")
        tp_done = sem("tp_done")
        tp_hi = sem("tp_hi")
        tp_lo = sem("tp_lo")
        f1_done = sem("f1_done")
        sil_done = sem("sil_done")
        ha_ready = sem("ha_ready")
        f23_done = sem("f23_done")
        gelu_done = sem("gelu_done")
        hi1_ready = sem("hi1_ready")
        hi23_ready = sem("hi23_ready")
        lo_ready = sem("lo_ready")
        f4_done = sem("f4_done")
        f4_out = sem("f4_out")
        ln2_in = sem("ln2_in")
        ln2_root = sem("ln2_root")
        y2_ready = sem("y2_ready")
        res2 = sem("res2")
        stored = sem("stored")

        block = ctx.enter_context(nc.Block())
        passed = {nc.vector.engine: sem("passed_dve"), nc.gpsimd.engine: sem("passed_pool")}

        def wait_alone(eng, semaphore, value):
            eng.wait_ge(semaphore, value)
            eng.sem_inc(passed[eng.engine], 1)

        def g_vg(t, j):
            return t * NG + (7 + j)

        def g_next(t, j):
            return t * NG + (15 + j)

        @block.sync
        def _(sp):
            sp.dma_start(raw_attn, w_attn).then_inc(wraw_in, 16)
            sp.dma_start(raw_o, w_o).then_inc(wraw_in, 16)
            sp.dma_start(xs[:], xT[0]).then_inc(x_in, 16)
            sp.dma_start(cst[:], consts).then_inc(consts_in, 16)
            sp.dma_start(raw_gk1, gk1).then_inc(consts_in, 16)
            sp.dma_start(masks[:], level_mask).then_inc(consts_in, 16)
            sp.dma_start(gk2_sb[:], gk2).then_inc(consts_in, 16)
            sp.dma_start(gkb_sb[:], gk_b).then_inc(consts_in, 16)
            sp.dma_start(rms[:], rms_w.partition_broadcast(P)).then_inc(consts_in, 16)
            sp.dma_start(w3s[:], w3_s.partition_broadcast(P)).then_inc(consts_in, 16)
            sp.dma_start(scales[:], s_in).then_inc(consts_in, 16)
            sp.dma_start(dw[:, 0:N123], w123).then_inc(copied, 16)
            sp.dma_start(dw[:, N123:N123 + NH], wh1).then_inc(copied, 16)
            sp.dma_start(dw[:, N123 + NH:], wh2).then_inc(copied, 16)
            sp.wait_ge(copied, 48)
            sp.dma_start(w123r[:].bitcast(F32), dw[:, 0:N123]).then_inc(w123_in, 16)

            def stage_piece(t, i, free=True):
                if free:
                    sp.wait_ge(checked, t * LOOKS + i - 1)
                sp.dma_start(stage[:, i % 2, :], dw[:, bass.ds(t * LOOKS * CW + i * CW, CW)]).then_inc(stage_in[i % 2], 16)

            def tile_loads(t, more_x=True, first=False):
                stage_piece(t, 0, free=not first)
                stage_piece(t, 1, free=not first)
                if more_x:
                    sp.wait_ge(x_split, t + 1)
                    sp.dma_start(xs[:], xT[bass.ds(t + 1, 1)].rearrange("o p c n -> (o p) c n")).then_inc(x_in, 16)
                if not first:
                    sp.wait_ge(y_out, t * B)
                sp.dma_start(xtok[:], x[:, bass.ds(t * C, C), :].rearrange("b p d -> p b d")).then_inc(xtok_in, 16)
                stage_piece(t, 2)
                stage_piece(t, 3)

            tile_loads(0, first=True)
            with sp.Fori(1, NT - 1) as t:
                tile_loads(t)
            tile_loads(NT - 1, more_x=False)
            sp.wait_ge(g_done, g_vg(NT - 1, 8))
            sp.wait_ge(flag_done, 1)
            sp.dma_start(wh1r[:].bitcast(F32), dw[:, N123:N123 + NH].rearrange("p (c n) -> p c n", c=MC)).then_inc(wh1_in, 16)
            sp.wait_ge(st_done, NT * B)
            sp.wait_ge(st_out, NT * B)
            sp.dma_start(wh2r[:].bitcast(F32), dw[:, N123 + NH:].rearrange("p (c n) -> p c n", c=MC)).then_inc(wh2_in, 16)
            with sp.Fori(0, NT) as t:
                sp.wait_ge(y2_ready, t + 1)
                sp.dma_start(out[:, bass.ds(t * C, C), :].rearrange("b p d -> p b d"),
                             x1_tile(t).rearrange("p (b d) -> p b d", b=B)).then_inc(stored, 16)
            sp.wait_ge(stored, 16 * NT)

        @block.tensor
        def _(pe):
            def split_product(dst, pairs):
                n = 3 * len(pairs)
                i = 0
                for w_hi, w_lo, x_h, x_l in pairs:
                    for a, b in ((w_hi, x_h), (w_hi, x_l), (w_lo, x_h)):
                        last = nc.tensor.matmul(dst, a, b, start=i == 0, stop=i == n - 1)
                        i += 1
                return last

            def feature_group(n, j, t_is_first=False):
                if not (t_is_first and j < 3):
                    pe.wait_ge(g_out, n - 2)
                bank = bank_g[j % 3]
                if j == 0:
                    last = split_product(ps[:, bank, :], [
                        (gk1_hi[:, c, :], gk1_lo[:, c, :], x_hi[:, c, :], x_lo[:, c, :]) for c in range(KC)])
                elif j < 3:
                    pe.wait_ge(g_out, n - j + 1)
                    m = j - 1
                    last = nc.tensor.matmul(ps[:, bank, :], gk2_sb[:, m * P:(m + 1) * P], r_sb,
                                            start=True, stop=True)
                else:
                    off = (j - 3) * P
                    last = split_product(ps[:, bank, :], [
                        (wa_hi[:, c, off:off + P], wa_lo[:, c, off:off + P], x_hi[:, c, :], x_lo[:, c, :])
                        for c in range(KC)])
                last.then_inc(g_done, 1)

            def token_group(t, j):
                pe.wait_ge(g_out, g_vg(t, j) - 2)
                b = j % B
                off = 2 * D if j < B else 4 * D
                last = split_product(ps[:, bank_g[(7 + j) % 3], :], [
                    (x_hi[:, c, b * C:(b + 1) * C], x_lo[:, c, b * C:(b + 1) * C],
                     wa_hi[:, c, off:off + DV], wa_lo[:, c, off:off + DV]) for c in range(KC)])
                last.then_inc(g_done, 1)

            def level(t, l, first=False):
                s = 1 << l
                for hp in range(HP):
                    pe.wait_ge(q_ready, t * NQ + HP * l + hp + 1)
                    if l == 0:
                        pe.wait_ge(g_out, t * NG + 7)
                        if hp == 0 and not first:
                            pe.wait_ge(st_out, t * B)
                    else:
                        pe.wait_ge(k_ready, t * NL + HP * (l - 1) + hp + 1)
                        pe.wait_ge(lev_out, t * NL + HP * (l - 1) + hp + 1)
                    for b in range(B):
                        g = hp * B + b
                        right = q2[:, g, :, :].rearrange("p h (n s) -> p h n s", s=2 * s)[:, :, :, s:2 * s]
                        last = nc.tensor.matmul(ps[:, bank_s[hp], b * C:(b + 1) * C], k[:, g, :], right,
                                                start=True, stop=True)
                    last.then_inc(lev_done, 1)

            def diag(t):
                pe.wait_ge(qk_ready, t + 1)
                for g in range(G):
                    last = nc.tensor.matmul(ps[:, bank_x, 2 * g:2 * g + 2], qk[:, g, :], select,
                                            start=True, stop=True)
                last.then_inc(diag_done, 1)

            def transpose_o(t, b):
                if b == 0:
                    pe.wait_ge(diag_out, t + 2)
                else:
                    pe.wait_ge(ogt_lo_out, t * B + b)
                pe.wait_ge(og_ready, t * B + b + 1)
                for h in range(H):
                    last = nc.tensor.transpose(ps[:, bank_x, h * P:(h + 1) * P],
                                               og[:, b, h * P:(h + 1) * P], ident)
                last.then_inc(ogt_done, 1)

            def project_o(t, b):
                pe.wait_ge(ogt_lo_out, t * B + b + 1)
                if b >= 2:
                    pe.wait_ge(y_out, t * B + b - 1)
                split_product(ps[:, bank_o[b % 2], 0:D], [
                    (ogt_hi[:, h, :], ogt_lo[:, h, :], wo_hi[:, h, :], wo_lo[:, h, :])
                    for h in range(H)]).then_inc(wo_done, 1)

            def transpose_k(t):
                for hp in range(HP):
                    pe.wait_ge(lev_out, t * NL + NL - HP + hp + 1)
                    pe.wait_ge(k_ready, t * NL + NL - HP + hp + 1)
                    for b in range(B):
                        g = hp * B + b
                        last = nc.tensor.transpose(ps[:, bank_s[hp], b * P:(b + 1) * P], k[:, g, :], ident)
                    last.then_inc(kt_done, 1)

            def attend(t, b, first):
                if b == 0:
                    pe.wait_ge(q_ready, t * NQ + NQ)
                    pe.wait_ge(g_out, g_vg(t, 3) + 1)
                    pe.wait_ge(diag_out, t + 1)
                    if first:
                        pe.wait_ge(zeroed, 4)
                    else:
                        pe.wait_ge(y_out, t * B)
                        pe.wait_ge(st_out, t * B)
                if b >= 2:
                    pe.wait_ge(o_out, t * B + b - 1)
                for hp in range(HP):
                    g = hp * B + b
                    for par in range(2):
                        h = 2 * hp + par
                        dst = ps[:, bank_o[b % 2], h * HV:(h + 1) * HV]
                        nc.tensor.matmul(dst, q2[:, g, par, :], state[:, g, par, :], start=True, stop=False)
                        last = nc.tensor.matmul(dst, att[:, g, par, :], v[:, b, h * HV:(h + 1) * HV],
                                                start=False, stop=True)
                last.then_inc(o_done, 1)

            def new_state(t, b):
                pe.wait_ge(kt_out, t * HP + HP)
                if b >= 2:
                    pe.wait_ge(st_out, t * B + b - 1)
                for hp in range(HP):
                    g = hp * B + b
                    last = nc.tensor.matmul(ps[:, bank_s[b % 2], hp * 2 * HV:(hp + 1) * 2 * HV], kt[:, g, :],
                                            v[:, b, hp * 2 * HV:(hp + 1) * 2 * HV], start=True, stop=True)
                last.then_inc(st_done, 1)

            def tile(t, first=False, last=False):
                level(t, 0, first)
                diag(t)
                token_group(t, 0)
                level(t, 1)
                if not first:
                    transpose_o(t - 1, 0)
                token_group(t, 1)
                for b in range(3):
                    level(t, 2 + b)
                    if not first:
                        project_o(t - 1, b)
                        transpose_o(t - 1, b + 1)
                    token_group(t, 2 + b)
                level(t, 5)
                if not first:
                    project_o(t - 1, 3)
                token_group(t, 5)
                level(t, 6)
                token_group(t, 6)
                token_group(t, 7)
                transpose_k(t)
                nxt = (lambda j: None) if last else (lambda j: feature_group(g_next(t, j), j))
                attend(t, 0, first)
                if not last:
                    pe.wait_ge(x_split, t + 2)
                nxt(0)
                new_state(t, 0)
                attend(t, 1, first)
                nxt(1)
                nxt(2)
                new_state(t, 1)
                attend(t, 2, first)
                nxt(3)
                new_state(t, 2)
                attend(t, 3, first)
                nxt(4)
                nxt(5)
                nxt(6)
                new_state(t, 3)

            pe.wait_ge(consts_in, 8 * 16)
            pe.wait_ge(gk1_split, 2)
            pe.wait_ge(x_split, 1)
            feature_group(0, 0, True)
            feature_group(1, 1, True)
            feature_group(2, 2, True)
            pe.wait_ge(w_split, 1)
            for j in range(3, 7):
                feature_group(j, j)
            tile(0, first=True)
            with pe.Fori(1, NT - 1) as t:
                tile(t)
            tile(NT - 1, last=True)
            for b in range(B):
                pe.wait_ge(og_ready, (NT - 1) * B + b + 1)
                if b:
                    pe.wait_ge(ogt_lo_out, (NT - 1) * B + b)
                for h in range(H):
                    last = nc.tensor.transpose(ps[:, bank_x, h * P:(h + 1) * P],
                                               og[:, b, h * P:(h + 1) * P], ident)
                last.then_inc(ogt_done, 1)
                project_o(NT - 1, b)

            def ffn(exact):
                as_is = (lambda a: a) if exact else (lambda a: a.bitcast(F32))

                def product(dst, w, h_hi, h_lo, m, ready):
                    n = w.shape[1]
                    for c in range(n):
                        ready(c)
                        for half in (h_hi, h_lo):
                            last = nc.tensor.matmul(
                                dst, as_is(w[:, c, m * P:(m + 1) * P]), as_is(half[:, c, :]),
                                start=c == 0 and half is h_hi, stop=c == n - 1 and half is h_lo)
                    return last

                def transpose_x1(t):
                    pe.wait_ge(xcur_ready, t + 1)
                    for c in range(KC):
                        for b in range(B):
                            last = nc.tensor.transpose(ps[:, 6 + c, b * C:(b + 1) * C],
                                                       xcur[:, b, c * P:(c + 1) * P], ident)
                        last.then_inc(tp_done, 1)

                def ffn_tile(t, first=False, last=False):
                    for m in range(MC):
                        if m < 2:
                            if not first:
                                pe.wait_ge(gelu_done, t * 2 * MC - 2 + 2 * m)
                        else:
                            pe.wait_ge(ha_ready, t * MC + m - 1)
                        def ready(c):
                            if m == 0:
                                pe.wait_ge(tp_lo, t * KC + c + 1)
                        product(ps[:, 2 * (m % 2), :], w1r, x1t_hi, x1t_lo, m, ready)
                        product(ps[:, 2 * (m % 2) + 1, :], w2r, x1t_hi, x1t_lo, m,
                                lambda c: None).then_inc(f1_done, 1)
                    if first:
                        pe.wait_ge(wh1_in, 16)
                    for m in range(MC):
                        if m < 4:
                            pe.wait_ge(ha_ready, t * MC + MC - 1 + m // 2)
                        else:
                            pe.wait_ge(gelu_done, t * 2 * MC + m - 3)
                        def ready(c):
                            if m == 0:
                                pe.wait_ge(lo_ready, t * 3 * MC + c + 1)
                        product(ps[:, m % 4, :], wh1r, ha_hi, ha_lo, m, ready).then_inc(f23_done, 1)
                    if first:
                        pe.wait_ge(wh2_in, 16)
                    if not last:
                        transpose_x1(t + 1)
                    for m in range(MC):
                        pe.wait_ge(gelu_done, t * 2 * MC + MC + m - 3)
                        def ready(c):
                            if m == 0:
                                pe.wait_ge(lo_ready, t * 3 * MC + MC + c + 1)
                        product(ps[:, m % 4, :], wh2r, hb_hi, hb_lo, m, ready).then_inc(f23_done, 1)
                    for b in range(B):
                        if not (first and b < 2):
                            pe.wait_ge(f4_out, t * B + b - 1)
                        i = 0
                        for c in range(MC):
                            if b == 0:
                                pe.wait_ge(lo_ready, t * 3 * MC + 2 * MC + c + 1)
                            for half in (ha_hi, ha_lo):
                                mm = nc.tensor.matmul(
                                    ps[:, 4 + b % 2, 0:D], as_is(half[:, c, b * C:(b + 1) * C]),
                                    as_is(w3r[:, c, :]), start=i == 0, stop=i == 2 * MC - 1)
                                i += 1
                        mm.then_inc(f4_done, 1)

                transpose_x1(0)
                ffn_tile(0, first=True)
                with pe.Fori(1, NT - 1) as t:
                    ffn_tile(t)
                ffn_tile(NT - 1, last=True)

            pe.wait_ge(x1_done, NT)
            pe.wait_ge(w123_in, 16)
            pe.wait_ge(flag_done, 1)
            odd_weights = pe.value_load(flag_i[0:1, 0:1], min_val=0, max_val=1)
            with pe.If(odd_weights == 0):
                ffn(True)
            with pe.Else():
                ffn(False)

        @block.scalar
        def _(act):
            chain = [0]

            def evacuate(n, j, dst, func, **kw):
                act.wait_ge(g_done, n + 1)
                nc.scalar.activation(dst, ps[0:dst.shape[0], bank_g[j % 3], :], func, **kw).then_inc(g_out, 1)

            def half(hp):
                return slice(hp * B, (hp + 1) * B)

            def feature_out(n, j, t=None):
                if j == 0:
                    if t is not None:
                        act.wait_ge(x1_done, t)
                    evacuate(n, j, r_sb, ACT.Copy)
                elif j < 3:
                    evacuate(n, j, gl[:, half(j - 1), :].rearrange("p b c -> p (b c)"), ACT.Identity,
                             bias=gkb_sb[:, j - 1:j])
                elif j < 5:
                    evacuate(n, j, q[:, half(j - 3), :].rearrange("p b c -> p (b c)"), ACT.Copy,
                             scale=HK ** -0.5)
                else:
                    evacuate(n, j, k[:, half(j - 5), :].rearrange("p b c -> p (b c)"), ACT.Copy)

            def softplus(t, n, first=False):
                act.preload_act_table_set("natural_log_exp_and_others")
                act.wait_ge(g_out, n)
                if not first:
                    act.wait_ge(diag_done, t)
                nc.scalar.activation(ex[:], gl[:], ACT.Abs).then_inc(act_chain, 1)
                act.wait_ge(act_chain, t * 2 + 1)
                nc.scalar.activation(ex[:], ex[:], ACT.Exp, scale=-1.0).then_inc(act_chain, 1)
                act.wait_ge(act_chain, t * 2 + 2)
                nc.scalar.activation(ex[:], ex[:], ACT.Ln, bias=1.0).then_inc(ln_g, 1)

            def decays(t):
                act.wait_ge(neg_g, t + 1)
                nc.scalar.activation(decay[:], ex[:], ACT.Exp, scale=1.0 / GATE_NORM).then_inc(decay_ready, 1)

            def hi_o(t, b):
                act.wait_ge(ogt_done, t * B + b + 1)
                nc.scalar.activation(ogt_hi[:].rearrange("p h c -> p (h c)"), ps[:, bank_x, :],
                                     ACT.Copy).then_inc(ogt_hi_out, 1)

            def v_out(t, b):
                evacuate(g_vg(t, b), 7 + b, v[:, b, :], ACT.Copy)

            def gate_out(t, b):
                evacuate(g_vg(t, 4 + b), 11 + b, gate[:, b, :], ACT.Silu)

            def square(t, b):
                act.wait_ge(o_done, t * B + b + 1)
                if b:
                    act.wait_ge(o_out, t * B + b)
                nc.scalar.activation(sq[:], ps[:, bank_o[b % 2], :], ACT.Square).then_inc(sq_done, 1)

            def tile(t, first=False, last=False):
                v_out(t, 0)
                if not first:
                    hi_o(t - 1, 0)
                for b in range(1, 4):
                    v_out(t, b)
                    if not first:
                        hi_o(t - 1, b)
                for b in range(4):
                    gate_out(t, b)
                if not first:
                    act.wait_ge(ln_in, t)
                    nc.scalar.activation(sdev, vare, ACT.Sqrt).then_inc(ln_root, 1)
                for hp in range(HP):
                    act.wait_ge(kt_done, t * HP + hp + 1)
                    nc.scalar.activation(kt[:, half(hp), :].rearrange("p b c -> p (b c)"),
                                         ps[:, bank_s[hp], :], ACT.Copy).then_inc(kt_out, 1)
                nxt = (lambda j: None) if last else (lambda j: feature_out(g_next(t, j), j, None if first else t))
                square(t, 0)
                nxt(0)
                square(t, 1)
                nxt(1)
                nxt(2)
                if not last:
                    softplus(t + 1, g_next(t, 3))
                square(t, 2)
                nxt(3)
                if not last:
                    decays(t + 1)
                square(t, 3)
                nxt(4)
                nxt(5)
                nxt(6)
                act.wait_ge(rms_in, t + 1)
                nc.scalar.activation(sroot, smean, ACT.Sqrt).then_inc(rms_root, 1)

            act.wait_ge(consts_in, 8 * 16)
            for j in range(3):
                feature_out(j, j)
            softplus(0, 3, first=True)
            for j in range(3, 7):
                feature_out(j, j)
            decays(0)
            tile(0, first=True)
            with act.Fori(1, NT - 1) as t:
                tile(t)
            tile(NT - 1, last=True)
            for b in range(B):
                hi_o(NT - 1, b)
            act.wait_ge(ln_in, NT)
            nc.scalar.activation(sdev, vare, ACT.Sqrt).then_inc(ln_root, 1)

            def x1_hi(t):
                for c in range(KC):
                    act.wait_ge(tp_done, t * KC + c + 1)
                    nc.scalar.activation(x1t_hi[:, c, :], ps[:, 6 + c, :], ACT.Copy).then_inc(tp_hi, 1)

            def hi_part(t, m):
                act.wait_ge(ha_ready, t * MC + m + 1)
                nc.scalar.activation(ha_hi[:, m, :], hf[:, m % 2, :], ACT.Copy).then_inc(hi1_ready, 1)

            def gelu(t, layer, m):
                j = layer * MC + m
                act.wait_ge(f23_done, t * 2 * MC + (j - MC) + 1)
                act.wait_ge(lo_ready, t * 3 * MC + j - 1)
                nc.scalar.activation(hf[:, m % 2, :], ps[:, m % 4, :], ACT.Gelu,
                                     scale=scales[:, layer + 1, m:m + 1]).then_inc(gelu_done, 1)

            def ffn_tile(t, first=False, last=False):
                for m in range(MC):
                    act.wait_ge(f1_done, t * MC + m + 1)
                    if not (first and m < 2):
                        act.wait_ge(ha_ready, t * MC + m - 1)
                    nc.scalar.activation(sil[:, m % 2, :], ps[:, 2 * (m % 2), :], ACT.Silu,
                                         scale=scales[:, 0, m:m + 1]).then_inc(sil_done, 1)
                    if m:
                        hi_part(t, m - 1)
                hi_part(t, MC - 1)
                for m in range(MC):
                    gelu(t, 1, m)
                if not last:
                    x1_hi(t + 1)
                for m in range(MC):
                    gelu(t, 2, m)
                act.wait_ge(ln2_in, t + 1)
                nc.scalar.activation(sdev, vare, ACT.Sqrt).then_inc(ln2_root, 1)

            x1_hi(0)
            ffn_tile(0, first=True)
            with act.Fori(1, NT - 1) as t:
                ffn_tile(t)
            ffn_tile(NT - 1, last=True)

        @block.vector
        def _(dve):
            def split_x(t):
                dve.wait_ge(x_in, t * 16 + 16)
                nc.vector.tensor_copy(x_hi[:], xs[:]).then_inc(xh_done, 1)
                dve.wait_ge(xh_done, t + 1)
                nc.vector.tensor_tensor(x_lo[:], xs[:], x_hi[:].bitcast(F32), ALU.subtract).then_inc(x_split, 1)

            def start_q(t, n_q):
                dve.wait_ge(g_out, n_q)
                dve.wait_ge(decay_ready, t + 1)
                for hp in range(HP):
                    for par in range(2):
                        rows, gs = slice(par * HK, (par + 1) * HK), slice(hp * B, (hp + 1) * B)
                        op = nc.vector.tensor_tensor(q2[rows, gs, par, :], q[rows, gs, :], decay[rows, gs, :],
                                                     ALU.mult)
                    op.then_inc(q_ready, 1)

            def level(t, l, first=False):
                s = 1 << l
                n = C // (2 * s)
                for hp in range(HP):
                    gs = slice(hp * B, (hp + 1) * B)
                    dve.wait_ge(lev_done, t * NL + HP * l + hp + 1)
                    dve.wait_ge(q_ready, t * NQ + HP * l + hp + 1)
                    if l or hp or not first:
                        dve.wait_ge(lev_out, t * NL + HP * l + hp)
                    if l == 1:
                        dve.wait_ge(diag_out, t + 1)
                    if l:
                        dve.wait_ge(tot_ready, t * LEVELS + l)
                    for par in range(2):
                        rows = slice(par * HK, (par + 1) * HK)
                        left = total(l)[rows, gs].rearrange("p g (n two) -> p g n two", two=2)[:, :, :, 0:1]
                        right = q2[rows, gs, par, :].rearrange("p g (n s) -> p g n s", s=2 * s)[:, :, :, s:2 * s]
                        op = nc.vector.tensor_tensor(right, right, left.to_broadcast([HK, B, n, s]), ALU.mult)
                    op.then_inc(q_ready, 1)
                    dst = att[:, gs, :, :].rearrange("p g h (n s) -> p (g h) n s", s=2 * s)[:, :, :, s:2 * s]
                    src = ps[:, bank_s[hp], :].rearrange("p (g n s) -> p g n s", n=n, s=s)
                    msk = masks[:, l, :].bitcast(I32).rearrange("p (o n s) -> p o n s", o=1, s=s)
                    nc.vector.copy_predicated(dst, msk.to_broadcast([P, 2 * B, n, s]), src).then_inc(lev_out, 1)

            def diagonal(t):
                dve.wait_ge(lev_out, t * NL + HP)
                wait_alone(dve, diag_done, t + 1)
                src = ps[:, bank_x, 0:2 * G].rearrange("p (g o) -> p g o", o=1)
                msk = ident.bitcast(I32).rearrange("p (o c) -> p o c", o=1)
                nc.vector.copy_predicated(att[:].rearrange("p g h c -> p (g h) c"),
                                          msk.to_broadcast([P, 2 * G, C]),
                                          src.to_broadcast([P, 2 * G, C])).then_inc(diag_out, 1)

            def normed_heads(t):
                dve.wait_ge(rms_root, t + 1)
                nc.vector.reciprocal(rrms, sroot).then_inc(rrms_done, 1)
                dve.wait_ge(rrms_done, t + 1)
                for b in range(B):
                    o_h = og[:, b, :].rearrange("p (h n) -> p h n", h=H)
                    sc = rrms[:, b * H:(b + 1) * H].rearrange("p (h o) -> p h o", o=1)
                    nc.vector.tensor_tensor(o_h, o_h, sc.to_broadcast([P, H, HV]), ALU.mult).then_inc(og_ready, 1)

            def lo_o(t, b):
                dve.wait_ge(ogt_hi_out, t * B + b + 1)
                nc.vector.tensor_tensor(ogt_lo[:].rearrange("p h c -> p (h c)"), ps[:, bank_x, :],
                                        ogt_hi[:].bitcast(F32).rearrange("p h c -> p (h c)"),
                                        ALU.subtract).then_inc(ogt_lo_out, 1)

            def residual(t, b):
                if b == 0:
                    dve.wait_ge(xtok_in, t * 16 + 16)
                dve.wait_ge(wo_done, t * B + b + 1)
                nc.vector.tensor_tensor(y[:, b, :], ps[:, bank_o[b % 2], 0:D], xtok[:, b, :],
                                        ALU.add).then_inc(y_out, 1)
                dve.wait_ge(y_out, t * B + b + 1)
                nc.vector.bn_stats(stats[:, b, :], y[:, b, :]).then_inc(st_stats, 1)
                wait_alone(dve, st_stats, t * B + b + 1)
                nc.vector.bn_aggr(mv[:, b, :], stats[:, b, :]).then_inc(st_aggr, 1)

            def var_eps(n_aggr, done):
                dve.wait_ge(st_aggr, n_aggr)
                nc.vector.tensor_scalar(vare, mv[:, :, 1:2].rearrange("p b o -> p (b o)"), EPS, None,
                                        ALU.add).then_inc(done, 1)

            def norm_rows(src, dst, n_root, root, last_sem, n_rstd):
                dve.wait_ge(root, n_root)
                nc.vector.reciprocal(rstd, sdev).then_inc(rstd_done, 1)
                dve.wait_ge(rstd_done, n_rstd)
                for b in range(B):
                    op = nc.vector.tensor_scalar(dst(b), src(b), mv[:, b, 0:1], rstd[:, b:b + 1],
                                                 ALU.subtract, ALU.mult)
                op.then_inc(last_sem, 1)

            def finish_x1(t):
                norm_rows(lambda b: y[:, b, :], lambda b: x1_row(t, b), t + 1, ln_root, x1_done, t + 1)

            def neg_gate(t):
                dve.wait_ge(ln_g, t + 1)
                nc.vector.scalar_tensor_tensor(ex[:], gl[:], 0.0, ex[:], ALU.min, ALU.subtract).then_inc(neg_g, 1)

            def heads_out(t, b):
                dve.wait_ge(gw_ready, t * B + b + 1)
                dve.wait_ge(sq_done, t * B + b + 1)
                nc.vector.tensor_tensor(og[:, b, :], ps[:, bank_o[b % 2], :], gate[:, b, :], ALU.mult)
                nc.vector.tensor_reduce(ssum[:, b * H:(b + 1) * H], sq[:].rearrange("p (h n) -> p h n", h=H),
                                        AX, ALU.add).then_inc(o_out, 1)

            def state_out(t, b):
                dve.wait_ge(st_done, t * B + b + 1)
                if b == 0:
                    dve.wait_ge(tot_ready, t * LEVELS + LEVELS)
                for hp in range(HP):
                    g = hp * B + b
                    for par in range(2):
                        rows = slice(par * HK, (par + 1) * HK)
                        s_old = state[rows, g, par, :]
                        add = ps[rows, bank_s[b % 2], (2 * hp + par) * HV:(2 * hp + par + 1) * HV]
                        op = nc.vector.scalar_tensor_tensor(s_old, s_old, total(LEVELS)[rows, g, :], add,
                                                            ALU.mult, ALU.add)
                op.then_inc(st_out, 1)

            def look(t, i):
                dve.wait_ge(rounded_done, t * LOOKS + i + 1)
                nc.vector.scalar_tensor_tensor(rounded[:].bitcast(F32), stage[:, i % 2, :], 1.0,
                                               rounded[:].bitcast(F32), ALU.mult, ALU.not_equal,
                                               accum_out=unequal[:, bass.ds(t * LOOKS + i, 1)]).then_inc(checked, 1)

            def tile(t, first=False, last=False):
                if first:
                    start_q(t, t * NG + 5)
                level(t, 0, first)
                if not first:
                    normed_heads(t - 1)
                diagonal(t)
                level(t, 1)
                if not first:
                    lo_o(t - 1, 0)
                for b in range(3):
                    level(t, 2 + b)
                    if not first:
                        residual(t - 1, b)
                        lo_o(t - 1, b + 1)
                level(t, 5)
                look(t, 0)
                if not first:
                    residual(t - 1, 3)
                    var_eps(t * B, ln_in)
                level(t, 6)
                if not last:
                    dve.wait_ge(g_done, g_vg(t, 8))
                    split_x(t + 1)
                if not first:
                    finish_x1(t - 1)
                heads_out(t, 0)
                state_out(t, 0)
                look(t, 1)
                heads_out(t, 1)
                state_out(t, 1)
                if not last:
                    neg_gate(t + 1)
                look(t, 2)
                heads_out(t, 2)
                state_out(t, 2)
                look(t, 3)
                heads_out(t, 3)
                if not last:
                    start_q(t + 1, g_next(t, 5))
                state_out(t, 3)
                dve.wait_ge(o_out, t * B + B)
                nc.vector.tensor_scalar(smean, ssum, 1.0 / HV, EPS, ALU.mult, ALU.add).then_inc(rms_in, 1)

            split_x(0)
            dve.wait_ge(wraw_in, 32)
            nc.vector.tensor_copy(wa_hi[:], raw_attn).then_inc(dve_chain, 1)
            nc.vector.tensor_copy(wo_hi[:], raw_o).then_inc(dve_chain, 1)
            dve.wait_ge(dve_chain, 2)
            nc.vector.tensor_tensor(wa_lo[:], raw_attn, wa_hi[:].bitcast(F32), ALU.subtract)
            nc.vector.tensor_tensor(wo_lo[:], raw_o, wo_hi[:].bitcast(F32), ALU.subtract).then_inc(w_split, 1)
            dve.wait_ge(consts_in, 8 * 16)
            dve.wait_ge(zeroed, 4)
            nc.vector.tensor_copy(gk1_hi[:, :, 0:LR], raw_gk1).then_inc(gk1_split, 1)
            dve.wait_ge(gk1_split, 1)
            nc.vector.tensor_tensor(gk1_lo[:, :, 0:LR], raw_gk1, gk1_hi[:, :, 0:LR].bitcast(F32),
                                    ALU.subtract).then_inc(gk1_split, 1)
            neg_gate(0)
            tile(0, first=True)
            with dve.Fori(1, NT - 1) as t:
                tile(t)
            tile(NT - 1, last=True)
            normed_heads(NT - 1)
            for b in range(B):
                lo_o(NT - 1, b)
                residual(NT - 1, b)
            var_eps(NT * B, ln_in)
            dve.wait_ge(checked, NCHECK)
            nc.vector.tensor_reduce(flag_p, unequal, AX, ALU.max).then_inc(flag_local, 1)
            dve.wait_ge(flag_all, 1)
            nc.vector.tensor_scalar(flag_i[:], flag_f, 0.0, None, ALU.is_gt).then_inc(flag_done, 1)
            finish_x1(NT - 1)

            def x1_lo(t):
                for c in range(KC):
                    dve.wait_ge(tp_hi, t * KC + c + 1)
                    nc.vector.tensor_tensor(x1t_lo[:, c, :], ps[:, 6 + c, :], x1t_hi[:, c, :].bitcast(F32),
                                            ALU.subtract).then_inc(tp_lo, 1)

            def lo_part(t, layer, m):
                dst = (ha_lo, hb_lo, ha_lo)[layer]
                hi = (ha_hi, hb_hi, ha_hi)[layer]
                if layer == 0:
                    dve.wait_ge(hi1_ready, t * MC + m + 1)
                else:
                    n = t * 2 * MC + (layer - 1) * MC + m + 1
                    dve.wait_ge(gelu_done, n)
                    nc.vector.tensor_copy(hi[:, m, :], hf[:, m % 2, :]).then_inc(hi23_ready, 1)
                    dve.wait_ge(hi23_ready, n)
                nc.vector.tensor_tensor(dst[:, m, :], hf[:, m % 2, :], hi[:, m, :].bitcast(F32),
                                        ALU.subtract).then_inc(lo_ready, 1)

            def ffn_tile(t, first=False, last=False):
                for m in range(MC):
                    dve.wait_ge(sil_done, t * MC + m + 1)
                    if m >= 2:
                        dve.wait_ge(lo_ready, t * 3 * MC + m - 1)
                    elif not first:
                        dve.wait_ge(y2_ready, t)
                    nc.vector.scalar_tensor_tensor(hf[:, m % 2, :], ps[:, 2 * (m % 2) + 1, :],
                                                   scales[:, 1, m:m + 1], sil[:, m % 2, :], ALU.mult,
                                                   ALU.mult).then_inc(ha_ready, 1)
                    if m:
                        lo_part(t, 0, m - 1)
                lo_part(t, 0, MC - 1)
                for m in range(MC):
                    lo_part(t, 1, m)
                if not last:
                    x1_lo(t + 1)
                for m in range(MC):
                    lo_part(t, 2, m)
                y2 = hf[:].rearrange("p a (c d) -> p (a c) d", d=D)
                for b in range(B):
                    dve.wait_ge(f4_done, t * B + b + 1)
                    if b == 0:
                        dve.wait_ge(lo_ready, t * 3 * MC + 3 * MC)
                    nc.vector.tensor_tensor(y2[:, b, :], ps[:, 4 + b % 2, 0:D], w3s[:], ALU.mult).then_inc(f4_out, 1)
                    dve.wait_ge(f4_out, t * B + b + 1)
                    nc.vector.tensor_tensor(y2[:, b, :], y2[:, b, :], x1_row(t, b), ALU.add).then_inc(res2, 1)
                    dve.wait_ge(res2, t * B + b + 1)
                    nc.vector.bn_stats(stats[:, b, :], y2[:, b, :]).then_inc(st_stats, 1)
                    wait_alone(dve, st_stats, t * B + (NT * B + b + 1))
                    nc.vector.bn_aggr(mv[:, b, :], stats[:, b, :]).then_inc(st_aggr, 1)
                var_eps(t * B + (NT * B + B), ln2_in)
                norm_rows(lambda b: y2[:, b, :], lambda b: x1_row(t, b), t + 1, ln2_root, y2_ready, t + (NT + 1))

            x1_lo(0)
            ffn_tile(0, first=True)
            with dve.Fori(1, NT - 1) as t:
                ffn_tile(t)
            ffn_tile(NT - 1, last=True)

        @block.gpsimd
        def _(pool):
            nc.gpsimd.memset(gk1_hi[:].bitcast(F32), 0.0)
            nc.gpsimd.memset(gk1_lo[:].bitcast(F32), 0.0).then_inc(zeroed, 1)
            nc.gpsimd.memset(q2[:], 0.0).then_inc(zeroed, 1)
            nc.gpsimd.memset(att[:], 0.0).then_inc(zeroed, 1)
            nc.gpsimd.memset(state[:], 0.0).then_inc(zeroed, 1)
            pool.wait_ge(consts_in, 8 * 16)

            def totals(t, l):
                if l == 1:
                    pool.wait_ge(decay_ready, t + 1)
                else:
                    pool.wait_ge(tot_ready, t * LEVELS + (l - 1))
                pairs = total(l - 1).rearrange("p g (n two) -> p g n two", two=2)
                dst = total(l).rearrange("p g (n o) -> p g n o", o=1)
                nc.gpsimd.tensor_tensor(dst, pairs[:, :, :, 0:1], pairs[:, :, :, 1:2],
                                        ALU.mult).then_inc(tot_ready, 1)

            def level(t, l):
                s = 1 << l
                n = C // (2 * s)
                right = total(l).rearrange("p g (n two) -> p g n two", two=2)[:, :, :, 1:2]
                left = k[:].rearrange("p g (n s) -> p g n s", s=2 * s)[:, :, :, 0:s]
                for hp in range(HP):
                    gs = slice(hp * B, (hp + 1) * B)
                    pool.wait_ge(lev_done, t * NL + HP * l + hp + 1)
                    if l:
                        pool.wait_ge(k_ready, t * NL + HP * (l - 1) + hp + 1)
                        pool.wait_ge(tot_ready, t * LEVELS + l)
                    else:
                        pool.wait_ge(qk_ready, t + 1)
                    nc.gpsimd.tensor_tensor(left[:, gs], left[:, gs], right[:, gs].to_broadcast([P, B, n, s]),
                                            ALU.mult).then_inc(k_ready, 1)

            def round_piece(t, i, free=True):
                wait_alone(pool, stage_in[i % 2], t * (LOOKS // 2 * 16) + (i // 2 + 1) * 16)
                if free:
                    wait_alone(pool, checked, t * LOOKS + i)
                nc.gpsimd.tensor_copy(rounded[:], stage[:, i % 2, :]).then_inc(rounded_done, 1)

            def tile(t, first=False):
                pool.wait_ge(g_out, t * NG + 7)
                pool.wait_ge(decay_ready, t + 1)
                nc.gpsimd.tensor_tensor(qk[:], q[:], k[:], ALU.mult).then_inc(qk_ready, 1)
                totals(t, 1)
                for l in range(LEVELS):
                    level(t, l)
                    if l + 2 <= LEVELS:
                        totals(t, l + 2)
                    if l == 4:
                        round_piece(t, 0, free=not first)
                for b in range(B):
                    pool.wait_ge(g_out, g_vg(t, 4 + b) + 1)
                    g_h = gate[:, b, :].rearrange("p (h n) -> p h n", h=H)
                    w_h = rms[:].rearrange("p (o n) -> p o n", o=1)
                    nc.gpsimd.tensor_tensor(g_h, g_h, w_h.to_broadcast([P, H, HV]), ALU.mult).then_inc(gw_ready, 1)
                for i in range(1, LOOKS):
                    round_piece(t, i)

            tile(0, first=True)
            with pool.Fori(1, NT) as t:
                tile(t)
            pool.wait_ge(flag_local, 1)
            nc.gpsimd.partition_all_reduce(flag_f, flag_p, P, bass.bass_isa.ReduceOp.max).then_inc(flag_all, 1)

            def copy_x1(t):
                nc.gpsimd.tensor_copy(xcur[:].rearrange("p b d -> p (b d)"), x1_tile(t)).then_inc(xcur_ready, 1)

            wait_alone(pool, x1_done, NT)
            copy_x1(0)
            with pool.Fori(1, NT) as t:
                wait_alone(pool, tp_done, t * KC)
                copy_x1(t)


_OUTS = [((B, T, D), "float32")]


def kernel(**inputs):
    import concourse.bacc as _bacc
    from concourse.bass_utils import run_bass_kernel_spmd as _run

    a = {n: np.ascontiguousarray(v) for n, v in inputs.items()}

    def rows(w, chunks):
        return w.reshape(chunks, P, -1).transpose(1, 0, 2)

    x = a["L0_attn_x"]
    attn = rows(np.concatenate([a["L0_attn_Wq"], a["L0_attn_Wk"], a["L0_attn_Wv"], a["L0_attn_Wg"]], axis=1), KC)
    flat = lambda w: w.reshape(P, -1)
    consts = np.zeros((P, P + 2), np.float32)
    consts[:, :P] = np.eye(P, dtype=np.float32)
    consts[:HK, -2] = 1.0
    consts[HK:, -1] = 1.0
    sent = {
        "x": x,
        "xT": x.reshape(B, NT, C, KC, P).transpose(1, 4, 3, 0, 2).reshape(NT, P, KC, TOK),
        "w_attn": attn,
        "w_o": rows(a["L0_attn_Wo"], H),
        "gk1": rows(a["L0_attn_gk_w1"], KC),
        "gk2": a["L0_attn_gk_w2"],
        "gk_b": a["L0_attn_gk_b"].reshape(HP, P).T,
        "rms_w": a["L0_attn_rms_w"],
        "w123": np.concatenate([flat(rows(a["L0_ffn_w1_w"].T, KC)), flat(rows(a["L0_ffn_w2_w"].T, KC)),
                                flat(rows(a["L0_ffn_w3_w"].T, MC))], axis=1),
        "wh1": flat(rows(a["L0_ffn_h1_w"].T, MC)),
        "wh2": flat(rows(a["L0_ffn_h2_w"].T, MC)),
        "s_in": np.stack([a[f"L0_ffn_{n}_s"].reshape(MC, P).T for n in ("w1", "w2", "h1", "h2")], axis=1),
        "w3_s": a["L0_ffn_w3_s"],
        "consts": consts,
        "level_mask": level_masks(),
    }
    nc = _bacc.Bacc("TRN2", target_bir_lowering=False, num_devices=1)
    arrays, args = {}, []
    for name, v in sent.items():
        v = np.ascontiguousarray(v)
        arrays[f"in_{name}"] = v
        args.append(nc.dram_tensor(f"in_{name}", v.shape, mybir.dt.from_np(v.dtype), kind="ExternalInput").ap())
    for i, (shape, dtype) in enumerate(_OUTS):
        args.append(nc.dram_tensor(f"out_{i}", shape, mybir.dt.from_np(np.dtype(dtype)), kind="ExternalOutput").ap())
    build(nc, *args)
    r = _run(nc, [arrays], core_ids=[0])
    return r.results[0]["out_0"]
```

```python
import numpy as np
import concourse.bass as bass
from concourse import mybir
from contextlib import ExitStack

F32 = mybir.dt.float32
F32R = mybir.dt.float32r
I32 = mybir.dt.int32
ALU = mybir.AluOpType
ACT = mybir.ActivationFunctionType
AX = mybir.AxisListType.X

P = 128
B, T, D = 4, 1024, 256
H, HK, HV = 4, 64, 128
LR = 16
DV = H * HV
C = 128
NT = T // C
TOK = B * C
KC = D // P
HP = H // 2
G = HP * B
LEVELS = 7
HID = 1024
MC = HID // P
EPS = 1e-5
GATE_NORM = 16.0
NQ = 1 + LEVELS
NL = HP * LEVELS
NG = 15
N123 = 2 * KC * HID + MC * D
NH = MC * HID
LOOKS = 4
NCHECK = NT * LOOKS
HALVES = ((0, B // 2), (B // 2, B))
WARM_UP = 4
CW = (N123 + 2 * NH) // NCHECK


def level_masks():
    m = np.zeros((P, LEVELS, 64), np.float32)
    for l in range(LEVELS):
        s = 1 << l
        for col in range(64):
            block = col // s
            m[2 * s * block:2 * s * block + s, l, col] = 1.0
    return m


def build(nc, x, xT, w_attn, w_o, gk1, gk2, gk_b, rms_w, w123, wh1, wh2, s_in, w3_s, consts, level_mask, out):
    ctx = ExitStack()
    with ctx:
        def sem(name):
            return ctx.enter_context(nc.semaphore(name))

        def sb_in(scope):
            return lambda name, shape, dt=F32: scope.enter_context(nc.sbuf_tensor(name, shape, dt))

        sb = sb_in(ctx)
        ps = ctx.enter_context(nc.psum_tensor("ps", [P, 8, 512], F32))
        bank_g = [0, 1, 2]
        bank_x = 3
        bank_o = [4, 5]
        bank_s = [6, 7]
        pair_1 = [0, 2, 6]

        x1 = sb("x1", [P, NT * B * D])

        def x1_tile(t):
            return x1[:, bass.ds(t * (B * D), B * D)]

        def x1_row(t, b):
            return x1[:, bass.ds(t * (B * D) + b * D, D)]

        w123r = sb("w123r", [P, 2 * KC * HID + MC * D], F32R)
        cst = sb("cst", [P, P + 2])
        w3s = sb("w3s", [P, D])
        scales = sb("scales", [P, 4, MC])
        small = sb("small", [P, 160])
        flag_i = sb("flag_i", [P, 1], I32)
        ident = cst[:, 0:P]
        select = cst[:, P:]
        stats = small[:, 0:24].rearrange("p (b s) -> p b s", b=B)
        mv = small[:, 24:32].rearrange("p (b s) -> p b s", b=B)
        rstd = small[:, 32:36]
        vare = small[:, 36:40]
        sdev = small[:, 40:44]
        ssum = small[:, 48:64]
        smean = small[:, 64:80]
        sroot = small[:, 80:96]
        rrms = small[:, 96:112]
        flag_p = small[:, 112:113]
        flag_f = small[:, 113:114]
        unequal = small[:, 120:120 + NCHECK]

        sa = ExitStack()
        a_ = sb_in(sa)
        wa_hi = a_("wa_hi", [P, KC, 6 * D], F32R)
        wa_lo = a_("wa_lo", [P, KC, 6 * D], F32R)
        xs = a_("xs", [P, KC, TOK])
        x_hi = a_("x_hi", [P, KC, TOK], F32R)
        x_lo = a_("x_lo", [P, KC, TOK], F32R)
        q = a_("q", [P, G, C])
        k = a_("k", [P, G, C])
        decay = a_("decay", [P, G, C])
        gl = a_("gl", [P, G, C])
        ex = a_("ex", [P, G, C])
        qk = ex
        tot = a_("tot", [P, G, C])
        q2 = a_("q2", [P, G, 2, C])
        att = a_("att", [P, G, 2, C])
        state = a_("state", [P, G, 2, HV])
        vg = a_("vg", [P, 2 * B * DV])
        v = vg[:, 0:B * DV].rearrange("p (b n) -> p b n", b=B)
        gate = vg[:, B * DV:].rearrange("p (b n) -> p b n", b=B)
        raw_attn = vg[:, 0:KC * 6 * D].rearrange("p (c n) -> p c n", c=KC)
        raw_o = vg[:, KC * 6 * D:].rearrange("p (h n) -> p h n", h=H)
        kt = a_("kt", [P, G, C])
        sq = a_("sq", [P, DV])
        gk1_hi = a_("gk1_hi", [P, KC, P], F32R)
        gk1_lo = a_("gk1_lo", [P, KC, P], F32R)
        gk2_sb = a_("gk2_sb", [LR, D])
        gkb_sb = a_("gkb_sb", [P, HP])
        masks = a_("masks", [P, LEVELS, 64])
        rms = a_("rms", [P, HV])
        rounded = a_("rounded", [P, CW], F32R)
        stage = a_("stage", [P, 2, CW])
        wo_hi = a_("wo_hi", [P, H, D], F32R)
        wo_lo = a_("wo_lo", [P, H, D], F32R)
        og = a_("og", [P, B, DV])
        ogt_hi = a_("ogt_hi", [P, H, P], F32R)
        ogt_lo = a_("ogt_lo", [P, H, P], F32R)
        xtok = a_("xtok", [P, B, D])
        y = a_("y", [P, B, D])
        raw_gk1 = y[:, 0, 0:KC * LR].rearrange("p (c n) -> p c n", c=KC)
        r_sb = y[0:LR, 2:4, :].rearrange("p b d -> p (b d)")
        sa.close()
        tot_at = {l: sum(G * (C >> m) for m in range(1, l)) for l in range(1, LEVELS + 1)}

        def total(l):
            n = C >> l
            if l == 0:
                return decay[:, :, :]
            flat = tot[:, :, :].rearrange("p g c -> p (g c)")
            return flat[:, tot_at[l]:tot_at[l] + G * n].rearrange("p (g n) -> p g n", g=G)

        sbs = ExitStack()
        b_ = sb_in(sbs)
        x1t_hi = b_("x1t_hi", [P, KC, TOK], F32R)
        x1t_lo = b_("x1t_lo", [P, KC, TOK], F32R)
        xcur = b_("xcur", [P, B, D])
        sil = b_("sil", [P, 2, TOK])
        hf = b_("hf", [P, 2, TOK])
        wh1r = b_("wh1r", [P, MC, HID], F32R)
        wh2r = b_("wh2r", [P, MC, HID], F32R)
        ha_hi = b_("ha_hi", [P, MC, TOK], F32R)
        ha_lo = b_("ha_lo", [P, MC, TOK], F32R)
        hb_hi = b_("hb_hi", [P, MC, TOK], F32R)
        hb_lo = b_("hb_lo", [P, MC, TOK], F32R)
        sbs.close()
        w1r = w123r[:, 0:KC * HID].rearrange("p (c n) -> p c n", c=KC)
        w2r = w123r[:, KC * HID:2 * KC * HID].rearrange("p (c n) -> p c n", c=KC)
        w3r = w123r[:, 2 * KC * HID:].rearrange("p (c n) -> p c n", c=MC)

        dw = nc.dram_tensor("dw", [P, N123 + 2 * NH], F32, kind="Internal").ap()

        consts_in = sem("consts_in")
        gates_in = sem("gates_in")
        wqk_in = sem("wqk_in")
        wrest_in = sem("wrest_in")
        w123_copied = sem("w123_copied")
        wh_copied = sem("wh_copied")
        w123_in = sem("w123_in")
        wh1_in = sem("wh1_in")
        wh2_in = sem("wh2_in")
        stage_in = [sem("stage_in0"), sem("stage_in1")]
        rounded_done = sem("rounded_done")
        checked = sem("checked")
        flag_done = sem("flag_done")
        warm_ready = sem("warm_ready")
        zeroed = sem("zeroed")
        gk1_split = sem("gk1_split")
        w_split = sem("w_split")
        x_in = sem("x_in")
        xtok_in = sem("xtok_in")
        x_split = sem("x_split")
        g_done = sem("g_done")
        g_out = sem("g_out")
        ln_g = sem("ln_g")
        neg_g = sem("neg_g")
        softplus_step = sem("softplus_step")
        w_hi = sem("w_hi")
        decay_ready = sem("decay_ready")
        q_ready = [sem("q_ready0"), sem("q_ready1")]
        k_ready = sem("k_ready")
        tot_ready = sem("tot_ready")
        qk_ready = sem("qk_ready")
        lev_done = sem("lev_done")
        lev_out = sem("lev_out")
        diag_done = sem("diag_done")
        diag_out = sem("diag_out")
        kt_done = sem("kt_done")
        kt_out = sem("kt_out")
        o_done = sem("o_done")
        sq_done = sem("sq_done")
        o_out = sem("o_out")
        gw_ready = sem("gw_ready")
        st_done = sem("st_done")
        st_out = sem("st_out")
        rms_in = sem("rms_in")
        rms_root = sem("rms_root")
        og_ready = sem("og_ready")
        ogt_done = sem("ogt_done")
        ogt_hi_out = sem("ogt_hi_out")
        ogt_lo_out = sem("ogt_lo_out")
        wo_done = sem("wo_done")
        y_out = sem("y_out")
        ln_in = sem("ln_in")
        ln_root = sem("ln_root")
        x1_done = sem("x1_done")
        xh_done = sem("xh_done")
        rrms_done = sem("rrms_done")
        st_stats = sem("st_stats")
        st_aggr = sem("st_aggr")
        rstd_done = sem("rstd_done")
        flag_local = sem("flag_local")
        flag_all = sem("flag_all")
        xcur_ready = sem("xcur_ready")
        tp_done = sem("tp_done")
        tp_hi = sem("tp_hi")
        tp_lo = sem("tp_lo")
        f1_done = sem("f1_done")
        sil_done = sem("sil_done")
        ha_ready = sem("ha_ready")
        f23_done = sem("f23_done")
        gelu_done = sem("gelu_done")
        hi1_ready = sem("hi1_ready")
        hi23_ready = sem("hi23_ready")
        lo_ready = sem("lo_ready")
        f4_done = sem("f4_done")
        f4_out = sem("f4_out")
        ln2_in = sem("ln2_in")
        ln2_root = sem("ln2_root")
        y2_ready = sem("y2_ready")
        res2 = sem("res2")
        stored = sem("stored")

        block = ctx.enter_context(nc.Block())
        passed = {nc.vector.engine: sem("passed_dve"), nc.gpsimd.engine: sem("passed_pool")}

        def wait_alone(eng, semaphore, value):
            eng.wait_ge(semaphore, value)
            eng.sem_inc(passed[eng.engine], 1)

        def g_vg(t, j):
            return t * NG + (7 + j)

        def g_next(t, j):
            return t * NG + (15 + j)

        @block.sync
        def _(sp):
            sp.dma_start(raw_gk1, gk1).then_inc(gates_in, 16)
            sp.dma_start(gk2_sb[:], gk2).then_inc(gates_in, 16)
            sp.dma_start(gkb_sb[:], gk_b).then_inc(gates_in, 16)
            sp.dma_start(xs[:], xT[0]).then_inc(x_in, 16)
            sp.dma_start(raw_attn[:, :, 0:2 * D], w_attn[:, :, 0:2 * D]).then_inc(wqk_in, 16)
            sp.dma_start(raw_attn[:, :, 2 * D:], w_attn[:, :, 2 * D:]).then_inc(wrest_in, 16)
            sp.dma_start(raw_o, w_o).then_inc(wrest_in, 16)
            sp.dma_start(cst[:], consts).then_inc(consts_in, 16)
            sp.dma_start(masks[:], level_mask).then_inc(consts_in, 16)
            sp.dma_start(rms[:], rms_w.partition_broadcast(P)).then_inc(consts_in, 16)
            sp.dma_start(w3s[:], w3_s.partition_broadcast(P)).then_inc(consts_in, 16)
            sp.dma_start(scales[:], s_in).then_inc(consts_in, 16)
            sp.dma_start(dw[:, 0:N123], w123).then_inc(w123_copied, 16)
            sp.wait_ge(w123_copied, 16)

            def stage_piece(t, i, free=True):
                if free:
                    sp.wait_ge(checked, t * LOOKS + i - 1)
                sp.dma_start(stage[:, i % 2, :],
                             dw[:, bass.ds(t * LOOKS * CW + i * CW, CW)]).then_inc(stage_in[i % 2], 16)

            def tile_loads(t, more_x=True, first=False):
                stage_piece(t, 0, free=not first)
                stage_piece(t, 1, free=not first)
                if more_x:
                    sp.wait_ge(x_split, t + 1)
                    sp.dma_start(xs[:], xT[bass.ds(t + 1, 1)].rearrange("o p c n -> (o p) c n")).then_inc(x_in, 16)
                else:
                    stage_piece(t, 2)
                    stage_piece(t, 3)
                if not first:
                    sp.wait_ge(y_out, t * B)
                sp.dma_start(xtok[:], x[:, bass.ds(t * C, C), :].rearrange("b p d -> p b d")).then_inc(xtok_in, 16)
                if more_x:
                    stage_piece(t, 2)
                    stage_piece(t, 3)

            tile_loads(0, first=True)
            sp.dma_start(w123r[:].bitcast(F32), dw[:, 0:N123]).then_inc(w123_in, 16)
            sp.dma_start(dw[:, N123:N123 + NH], wh1).then_inc(wh_copied, 16)
            sp.dma_start(dw[:, N123 + NH:], wh2).then_inc(wh_copied, 16)
            tile_loads(1)
            sp.wait_ge(wh_copied, 32)
            with sp.Fori(2, NT - 1) as t:
                tile_loads(t)
            tile_loads(NT - 1, more_x=False)
            sp.wait_ge(g_done, g_vg(NT - 1, 8))
            sp.wait_ge(lev_out, NT * NL)
            sp.dma_start(wh1r[:].bitcast(F32),
                         dw[:, N123:N123 + NH].rearrange("p (c n) -> p c n", c=MC)).then_inc(wh1_in, 16)
            sp.wait_ge(o_done, NT * B)
            sp.dma_start(wh2r[:].bitcast(F32),
                         dw[:, N123 + NH:].rearrange("p (c n) -> p c n", c=MC)).then_inc(wh2_in, 16)
            with sp.Fori(0, NT - 1) as t:
                sp.wait_ge(y2_ready, t + 1)
                sp.dma_start(out[:, bass.ds(t * C, C), :].rearrange("b p d -> p b d"),
                             x1_tile(t).rearrange("p (b d) -> p b d", b=B)).then_inc(stored, 16)
            last_rows = x1[:, (NT - 1) * B * D:].rearrange("p (b d) -> p b d", b=B)
            for i, (b0, b1) in enumerate(HALVES):
                sp.wait_ge(y2_ready, NT + i)
                sp.dma_start(out[b0:b1, (NT - 1) * C:, :].rearrange("b p d -> p b d"),
                             last_rows[:, b0:b1, :]).then_inc(stored, 16)
            sp.wait_ge(stored, 16 * (NT + 1))

        @block.tensor
        def _(pe):
            def split_product(dst, pairs):
                n = 3 * len(pairs)
                i = 0
                for w_hi, w_lo, x_h, x_l in pairs:
                    for a, b in ((w_hi, x_h), (w_hi, x_l), (w_lo, x_h)):
                        last = nc.tensor.matmul(dst, a, b, start=i == 0, stop=i == n - 1)
                        i += 1
                return last

            def feature_group(n, j, banks_new=False):
                if not (banks_new and j < 3):
                    pe.wait_ge(g_out, n - 2)
                bank = bank_g[j % 3]
                if j == 0:
                    last = split_product(ps[:, bank, :], [
                        (gk1_hi[:, c, :], gk1_lo[:, c, :], x_hi[:, c, :], x_lo[:, c, :]) for c in range(KC)])
                elif j < 3:
                    pe.wait_ge(g_out, n - j + 1)
                    m = j - 1
                    last = nc.tensor.matmul(ps[:, bank, :], gk2_sb[:, m * P:(m + 1) * P], r_sb,
                                            start=True, stop=True)
                else:
                    off = (j - 3) * P
                    last = split_product(ps[:, bank, :], [
                        (wa_hi[:, c, off:off + P], wa_lo[:, c, off:off + P], x_hi[:, c, :], x_lo[:, c, :])
                        for c in range(KC)])
                last.then_inc(g_done, 1)

            def token_group(t, j):
                pe.wait_ge(g_out, g_vg(t, j) - 2)
                b = j % B
                off = 2 * D if j < B else 4 * D
                last = split_product(ps[:, bank_g[(7 + j) % 3], :], [
                    (x_hi[:, c, b * C:(b + 1) * C], x_lo[:, c, b * C:(b + 1) * C],
                     wa_hi[:, c, off:off + DV], wa_lo[:, c, off:off + DV]) for c in range(KC)])
                last.then_inc(g_done, 1)

            def level(t, l, first=False):
                s = 1 << l
                for hp in range(HP):
                    pe.wait_ge(q_ready[hp], t * NQ + l + 1)
                    if l == 0:
                        pe.wait_ge(g_out, t * NG + 7)
                        if not first:
                            pe.wait_ge(st_out, t * B - 1 + hp)
                    else:
                        pe.wait_ge(k_ready, t * NL + HP * (l - 1) + hp + 1)
                        pe.wait_ge(lev_out, t * NL + HP * (l - 1) + hp + 1)
                    for b in range(B):
                        g = hp * B + b
                        right = q2[:, g, :, :].rearrange("p h (n s) -> p h n s", s=2 * s)[:, :, :, s:2 * s]
                        last = nc.tensor.matmul(ps[:, bank_s[hp], b * C:(b + 1) * C], k[:, g, :], right,
                                                start=True, stop=True)
                    last.then_inc(lev_done, 1)

            def diag(t):
                pe.wait_ge(qk_ready, t + 1)
                for g in range(G):
                    last = nc.tensor.matmul(ps[:, bank_x, 2 * g:2 * g + 2], qk[:, g, :], select,
                                            start=True, stop=True)
                last.then_inc(diag_done, 1)

            def transpose_o(t, b):
                if b == 0:
                    pe.wait_ge(diag_out, t + 2)
                else:
                    pe.wait_ge(ogt_lo_out, t * B + b)
                pe.wait_ge(og_ready, t * B + b + 1)
                for h in range(H):
                    last = nc.tensor.transpose(ps[:, bank_x, h * P:(h + 1) * P],
                                               og[:, b, h * P:(h + 1) * P], ident)
                last.then_inc(ogt_done, 1)

            def project_o(t, b):
                pe.wait_ge(ogt_lo_out, t * B + b + 1)
                if b >= 2:
                    pe.wait_ge(y_out, t * B + b - 1)
                split_product(ps[:, bank_o[b % 2], 0:D], [
                    (ogt_hi[:, h, :], ogt_lo[:, h, :], wo_hi[:, h, :], wo_lo[:, h, :])
                    for h in range(H)]).then_inc(wo_done, 1)

            def transpose_k(t):
                for hp in range(HP):
                    pe.wait_ge(lev_out, t * NL + NL - HP + hp + 1)
                    pe.wait_ge(k_ready, t * NL + NL - HP + hp + 1)
                    for b in range(B):
                        g = hp * B + b
                        last = nc.tensor.transpose(ps[:, bank_s[hp], b * P:(b + 1) * P], k[:, g, :], ident)
                    last.then_inc(kt_done, 1)

            def attend(t, b, first):
                if b == 0:
                    pe.wait_ge(q_ready[0], t * NQ + NQ)
                    pe.wait_ge(q_ready[1], t * NQ + NQ)
                    pe.wait_ge(g_out, g_vg(t, 3) + 1)
                    pe.wait_ge(diag_out, t + 1)
                    if first:
                        pe.wait_ge(zeroed, 4)
                    else:
                        pe.wait_ge(y_out, t * B)
                        pe.wait_ge(st_out, t * B)
                if b >= 2:
                    pe.wait_ge(o_out, t * B + b - 1)
                for hp in range(HP):
                    g = hp * B + b
                    for par in range(2):
                        h = 2 * hp + par
                        dst = ps[:, bank_o[b % 2], h * HV:(h + 1) * HV]
                        nc.tensor.matmul(dst, q2[:, g, par, :], state[:, g, par, :], start=True, stop=False)
                        last = nc.tensor.matmul(dst, att[:, g, par, :], v[:, b, h * HV:(h + 1) * HV],
                                                start=False, stop=True)
                last.then_inc(o_done, 1)

            def new_state(t, b):
                pe.wait_ge(kt_out, t * HP + HP)
                if b >= 2:
                    pe.wait_ge(st_out, t * B + b - 1)
                for hp in range(HP):
                    g = hp * B + b
                    last = nc.tensor.matmul(ps[:, bank_s[b % 2], hp * 2 * HV:(hp + 1) * 2 * HV], kt[:, g, :],
                                            v[:, b, hp * 2 * HV:(hp + 1) * 2 * HV], start=True, stop=True)
                last.then_inc(st_done, 1)

            def transpose_x1(src):
                for c in range(KC):
                    for b in range(B):
                        last = nc.tensor.transpose(ps[:, 6 + c, b * C:(b + 1) * C], src(b, c), ident)
                    last.then_inc(tp_done, 1)

            def tile(t, first=False, last=False):
                if first:
                    pe.wait_ge(w_split, 2)
                    pe.wait_ge(consts_in, 5 * 16)
                token_group(t, 0)
                level(t, 0, first)
                diag(t)
                token_group(t, 1)
                level(t, 1)
                token_group(t, 2)
                if not first:
                    transpose_o(t - 1, 0)
                for b in range(3):
                    level(t, 2 + b)
                    if not first:
                        project_o(t - 1, b)
                        transpose_o(t - 1, b + 1)
                    if b < 2:
                        token_group(t, 3 + b)
                level(t, 5)
                if not first:
                    project_o(t - 1, 3)
                token_group(t, 5)
                level(t, 6)
                token_group(t, 6)
                token_group(t, 7)
                if last:
                    pe.wait_ge(lev_out, NT * NL)
                    transpose_x1(lambda b, c: x1[:, b * D + c * P:b * D + (c + 1) * P])
                    for b in range(B):
                        attend(t, b, first)
                    return
                transpose_k(t)
                nxt = lambda j: feature_group(g_next(t, j), j)
                attend(t, 0, first)
                pe.wait_ge(x_split, t + 2)
                nxt(0)
                new_state(t, 0)
                attend(t, 1, first)
                nxt(1)
                nxt(2)
                new_state(t, 1)
                attend(t, 2, first)
                nxt(3)
                new_state(t, 2)
                attend(t, 3, first)
                nxt(4)
                new_state(t, 3)
                nxt(5)
                nxt(6)

            pe.wait_ge(warm_ready, 1)
            for _ in range(WARM_UP):
                nc.tensor.matmul(ps[:, bank_s[1], :], kt[:, 0, :], kt[:, 0:B, :].rearrange("p b c -> p (b c)"),
                                 start=True, stop=True)
            pe.wait_ge(gates_in, 3 * 16)
            pe.wait_ge(gk1_split, 2)
            pe.wait_ge(x_split, 1)
            feature_group(0, 0, True)
            feature_group(1, 1, True)
            feature_group(2, 2, True)
            pe.wait_ge(w_split, 1)
            for j in range(3, 7):
                feature_group(j, j)
            tile(0, first=True)
            with pe.Fori(1, NT - 1) as t:
                tile(t)
            tile(NT - 1, last=True)

            def ffn(exact):
                as_is = (lambda a: a) if exact else (lambda a: a.bitcast(F32))

                def product(dst, w, h_hi, h_lo, m, ready):
                    n = w.shape[1]
                    for c in range(n):
                        ready(c)
                        for half in (h_hi, h_lo):
                            last = nc.tensor.matmul(
                                dst, as_is(w[:, c, m * P:(m + 1) * P]), as_is(half[:, c, :]),
                                start=c == 0 and half is h_hi, stop=c == n - 1 and half is h_lo)
                    return last

                def last_heads(b):
                    pe.wait_ge(og_ready, (NT - 1) * B + b + 1)
                    if b == 0:
                        pe.wait_ge(o_out, NT * B)
                    else:
                        pe.wait_ge(ogt_lo_out, (NT - 1) * B + b)
                    for h in range(H):
                        last = nc.tensor.transpose(ps[:, bank_o[0], h * P:(h + 1) * P],
                                                   og[:, b, h * P:(h + 1) * P], ident)
                    last.then_inc(ogt_done, 1)

                def last_project(b):
                    pe.wait_ge(ogt_lo_out, (NT - 1) * B + b + 1)
                    if b:
                        pe.wait_ge(y_out, (NT - 1) * B + b)
                    split_product(ps[:, bank_o[1], 0:D], [
                        (ogt_hi[:, h, :], ogt_lo[:, h, :], wo_hi[:, h, :], wo_lo[:, h, :])
                        for h in range(H)]).then_inc(wo_done, 1)

                def ffn_tile(t, first=False, last=False):
                    for m in range(MC):
                        if m >= 3:
                            pe.wait_ge(ha_ready, t * MC + m - 2)
                        elif first and m == 0:
                            pe.wait_ge(g_out, NT * NG)
                            pe.wait_ge(diag_out, NT)
                            pe.wait_ge(ogt_lo_out, (NT - 1) * B)
                        elif m < 2 and not first:
                            pe.wait_ge(gelu_done, t * 2 * MC - 2 + 2 * m)
                        def ready(c):
                            if m == 0:
                                pe.wait_ge(tp_lo, t * KC + c + 1)
                        bank = pair_1[m % 3]
                        product(ps[:, bank, :], w1r, x1t_hi, x1t_lo, m, ready)
                        product(ps[:, bank + 1, :], w2r, x1t_hi, x1t_lo, m,
                                lambda c: None).then_inc(f1_done, 1)
                        if first and 3 <= m < 7:
                            last_project(m - 3)
                        if first and 2 <= m < 6:
                            last_heads(m - 2)
                    if first:
                        pe.wait_ge(wh1_in, 16)
                    for m in range(MC):
                        if m < 4:
                            pe.wait_ge(ha_ready, t * MC + MC - 1 + m // 2)
                        else:
                            pe.wait_ge(gelu_done, t * 2 * MC + m - 3)
                        def ready(c):
                            if m == 0:
                                pe.wait_ge(lo_ready, t * 3 * MC + c + 1)
                        product(ps[:, m % 4, :], wh1r, ha_hi, ha_lo, m, ready).then_inc(f23_done, 1)
                    if first:
                        pe.wait_ge(wh2_in, 16)
                    for m in range(MC):
                        pe.wait_ge(gelu_done, t * 2 * MC + MC + m - 3)
                        def ready(c):
                            if m == 0:
                                pe.wait_ge(lo_ready, t * 3 * MC + MC + c + 1)
                        product(ps[:, m % 4, :], wh2r, hb_hi, hb_lo, m, ready).then_inc(f23_done, 1)
                    if not last:
                        pe.wait_ge(xcur_ready, t + 1)
                        transpose_x1(lambda b, c: xcur[:, b, c * P:(c + 1) * P])
                    if first:
                        pe.wait_ge(y_out, NT * B)
                    for b in range(B):
                        if not (first and b < 2):
                            pe.wait_ge(f4_out, t * B + b - 1)
                        i = 0
                        for c in range(MC):
                            if b == 0:
                                pe.wait_ge(lo_ready, t * 3 * MC + 2 * MC + c + 1)
                            for half in (ha_hi, ha_lo):
                                mm = nc.tensor.matmul(
                                    ps[:, 4 + b % 2, 0:D], as_is(half[:, c, b * C:(b + 1) * C]),
                                    as_is(w3r[:, c, :]), start=i == 0, stop=i == 2 * MC - 1)
                                i += 1
                        mm.then_inc(f4_done, 1)

                ffn_tile(0, first=True)
                with pe.Fori(1, NT - 1) as t:
                    ffn_tile(t)
                ffn_tile(NT - 1, last=True)

            pe.wait_ge(w123_in, 16)
            pe.wait_ge(flag_done, 1)
            odd_weights = pe.value_load(flag_i[0:1, 0:1], min_val=0, max_val=1)
            with pe.If(odd_weights == 0):
                ffn(True)
            with pe.Else():
                ffn(False)

        @block.scalar
        def _(act):
            def evacuate(n, j, dst, func, **kw):
                act.wait_ge(g_done, n + 1)
                nc.scalar.activation(dst, ps[0:dst.shape[0], bank_g[j % 3], :], func, **kw).then_inc(g_out, 1)

            def half(hp):
                return slice(hp * B, (hp + 1) * B)

            def feature_out(n, j, t=None):
                if j == 0:
                    if t is not None:
                        act.wait_ge(x1_done, t)
                    evacuate(n, j, r_sb, ACT.Copy)
                elif j < 3:
                    evacuate(n, j, gl[:, half(j - 1), :].rearrange("p b c -> p (b c)"), ACT.Identity,
                             bias=gkb_sb[:, j - 1:j])
                elif j < 5:
                    evacuate(n, j, q[:, half(j - 3), :].rearrange("p b c -> p (b c)"), ACT.Copy,
                             scale=HK ** -0.5)
                else:
                    evacuate(n, j, k[:, half(j - 5), :].rearrange("p b c -> p (b c)"), ACT.Copy)

            def softplus(t, n, first=False):
                if not first:
                    act.preload_act_table_set("natural_log_exp_and_others")
                act.wait_ge(g_out, n)
                if not first:
                    act.wait_ge(diag_done, t)
                nc.scalar.activation(ex[:], gl[:], ACT.Abs).then_inc(softplus_step, 1)
                act.wait_ge(softplus_step, t * 2 + 1)
                nc.scalar.activation(ex[:], ex[:], ACT.Exp, scale=-1.0).then_inc(softplus_step, 1)
                act.wait_ge(softplus_step, t * 2 + 2)
                nc.scalar.activation(ex[:], ex[:], ACT.Ln, bias=1.0).then_inc(ln_g, 1)

            def decays(t):
                act.wait_ge(neg_g, t + 1)
                nc.scalar.activation(decay[:], ex[:], ACT.Exp, scale=1.0 / GATE_NORM).then_inc(decay_ready, 1)

            def hi_o(t, b):
                act.wait_ge(ogt_done, t * B + b + 1)
                nc.scalar.activation(ogt_hi[:].rearrange("p h c -> p (h c)"), ps[:, bank_x, :],
                                     ACT.Copy).then_inc(ogt_hi_out, 1)

            def v_out(t, b):
                evacuate(g_vg(t, b), 7 + b, v[:, b, :], ACT.Copy)

            def gate_out(t, b):
                evacuate(g_vg(t, 4 + b), 11 + b, gate[:, b, :], ACT.Silu)

            def square(t, b):
                act.wait_ge(o_done, t * B + b + 1)
                if b:
                    act.wait_ge(o_out, t * B + b)
                nc.scalar.activation(sq[:], ps[:, bank_o[b % 2], :], ACT.Square).then_inc(sq_done, 1)

            def x1_hi(t):
                for c in range(KC):
                    act.wait_ge(tp_done, t * KC + c + 1)
                    nc.scalar.activation(x1t_hi[:, c, :], ps[:, 6 + c, :], ACT.Copy).then_inc(tp_hi, 1)

            def root_heads(t):
                act.wait_ge(rms_in, t + 1)
                nc.scalar.activation(sroot, smean, ACT.Sqrt).then_inc(rms_root, 1)

            def normed_heads(t):
                act.wait_ge(rrms_done, t + 1)
                for b in range(B):
                    for h in range(H):
                        o_h = og[:, b, h * HV:(h + 1) * HV]
                        op = nc.scalar.activation(o_h, o_h, ACT.Copy, scale=rrms[:, b * H + h:b * H + h + 1])
                    op.then_inc(og_ready, 1)

            def round_piece(t, i, first=False):
                act.wait_ge(stage_in[i % 2], t * (LOOKS // 2 * 16) + (i // 2 + 1) * 16)
                if not first:
                    act.wait_ge(checked, t * LOOKS + i)
                nc.scalar.activation(rounded[:], stage[:, i % 2, :], ACT.Copy).then_inc(rounded_done, 1)

            def tile(t, first=False, last=False):
                v_out(t, 0)
                if not first:
                    root_heads(t - 1)
                    normed_heads(t - 1)
                v_out(t, 1)
                if last:
                    round_piece(t, 0)
                v_out(t, 2)
                if not first:
                    hi_o(t - 1, 0)
                    hi_o(t - 1, 1)
                v_out(t, 3)
                if last:
                    round_piece(t, 1)
                if not first:
                    hi_o(t - 1, 2)
                gate_out(t, 0)
                if last:
                    round_piece(t, 2)
                if not first:
                    hi_o(t - 1, 3)
                round_piece(t, 3 if last else 0, first)
                for b in range(1, 4):
                    gate_out(t, b)
                if not first:
                    act.wait_ge(ln_in, t)
                    nc.scalar.activation(sdev, vare, ACT.Sqrt).then_inc(ln_root, 1)
                if last:
                    x1_hi(0)
                    for b in range(B):
                        square(t, b)
                    return
                for hp in range(HP):
                    act.wait_ge(kt_done, t * HP + hp + 1)
                    nc.scalar.activation(kt[:, half(hp), :].rearrange("p b c -> p (b c)"),
                                         ps[:, bank_s[hp], :], ACT.Copy).then_inc(kt_out, 1)
                nxt = lambda j: feature_out(g_next(t, j), j, None if first else t)
                square(t, 0)
                nxt(0)
                round_piece(t, 1)
                square(t, 1)
                round_piece(t, 2)
                nxt(1)
                nxt(2)
                softplus(t + 1, g_next(t, 3))
                round_piece(t, 3)
                square(t, 2)
                nxt(3)
                decays(t + 1)
                square(t, 3)
                nxt(4)
                nxt(5)
                nxt(6)

            act.preload_act_table_set("natural_log_exp_and_others")
            act.wait_ge(gates_in, 3 * 16)
            for j in range(3):
                feature_out(j, j)
            softplus(0, 3, first=True)
            feature_out(3, 3)
            feature_out(4, 4)
            decays(0)
            feature_out(5, 5)
            feature_out(6, 6)
            tile(0, first=True)
            with act.Fori(1, NT - 1) as t:
                tile(t)
            tile(NT - 1, last=True)

            def hi_part(t, m):
                act.wait_ge(ha_ready, t * MC + m + 1)
                nc.scalar.activation(ha_hi[:, m, :], hf[:, m % 2, :], ACT.Copy).then_inc(hi1_ready, 1)

            def gelu(t, layer, m):
                j = layer * MC + m
                act.wait_ge(f23_done, t * 2 * MC + (j - MC) + 1)
                act.wait_ge(lo_ready, t * 3 * MC + j - 1)
                nc.scalar.activation(hf[:, m % 2, :], ps[:, m % 4, :], ACT.Gelu,
                                     scale=scales[:, layer + 1, m:m + 1]).then_inc(gelu_done, 1)

            def last_heads_hi(b):
                act.wait_ge(ogt_done, (NT - 1) * B + b + 1)
                nc.scalar.activation(ogt_hi[:].rearrange("p h c -> p (h c)"), ps[:, bank_o[0], :],
                                     ACT.Copy).then_inc(ogt_hi_out, 1)

            def root_y2(n, b0=0, b1=B):
                act.wait_ge(ln2_in, n)
                nc.scalar.activation(sdev[:, b0:b1], vare[:, b0:b1], ACT.Sqrt).then_inc(ln2_root, 1)

            def ffn_tile(t, first=False, last=False):
                for m in range(MC):
                    if first and m in (2, 4, 5, 6):
                        last_heads_hi(m - 3 if m > 2 else 0)
                    act.wait_ge(f1_done, t * MC + m + 1)
                    if not (first and m < 2):
                        act.wait_ge(ha_ready, t * MC + m - 1)
                    nc.scalar.activation(sil[:, m % 2, :], ps[:, pair_1[m % 3], :], ACT.Silu,
                                         scale=scales[:, 0, m:m + 1]).then_inc(sil_done, 1)
                    if m:
                        hi_part(t, m - 1)
                hi_part(t, MC - 1)
                if first:
                    act.wait_ge(ln_in, NT)
                    nc.scalar.activation(sdev, vare, ACT.Sqrt).then_inc(ln_root, 1)
                else:
                    root_y2(t)
                for m in range(MC):
                    gelu(t, 1, m)
                for m in range(MC):
                    gelu(t, 2, m)
                if not last:
                    x1_hi(t + 1)

            root_heads(NT - 1)
            ffn_tile(0, first=True)
            with act.Fori(1, NT - 1) as t:
                ffn_tile(t)
            ffn_tile(NT - 1, last=True)
            for i, (b0, b1) in enumerate(HALVES):
                root_y2(NT + i, b0, b1)

        @block.vector
        def _(dve):
            def split_x(t):
                dve.wait_ge(x_in, t * 16 + 16)
                nc.vector.tensor_copy(x_hi[:], xs[:]).then_inc(xh_done, 1)
                dve.wait_ge(xh_done, t + 1)
                nc.vector.tensor_tensor(x_lo[:], xs[:], x_hi[:].bitcast(F32), ALU.subtract).then_inc(x_split, 1)

            def start_q(t, hp, n_q):
                dve.wait_ge(g_out, n_q)
                dve.wait_ge(decay_ready, t + 1)
                for par in range(2):
                    rows, gs = slice(par * HK, (par + 1) * HK), slice(hp * B, (hp + 1) * B)
                    op = nc.vector.tensor_tensor(q2[rows, gs, par, :], q[rows, gs, :], decay[rows, gs, :],
                                                 ALU.mult)
                op.then_inc(q_ready[hp], 1)

            def raise_q(t, l):
                s = 1 << l
                n = C // (2 * s)
                dve.wait_ge(q_ready[0], t * NQ + l + 1)
                if l:
                    dve.wait_ge(tot_ready, t * LEVELS + l)
                for par in range(2):
                    rows, gs = slice(par * HK, (par + 1) * HK), slice(0, B)
                    left = total(l)[rows, gs].rearrange("p g (n two) -> p g n two", two=2)[:, :, :, 0:1]
                    right = q2[rows, gs, par, :].rearrange("p g (n s) -> p g n s", s=2 * s)[:, :, :, s:2 * s]
                    op = nc.vector.tensor_tensor(right, right, left.to_broadcast([HK, B, n, s]), ALU.mult)
                op.then_inc(q_ready[0], 1)

            def level(t, l, first=False):
                s = 1 << l
                n = C // (2 * s)
                for hp in range(HP):
                    gs = slice(hp * B, (hp + 1) * B)
                    wait = dve.wait_ge if hp == 0 else lambda semaphore, count: wait_alone(dve, semaphore, count)
                    wait(lev_done, t * NL + HP * l + hp + 1)
                    if l or hp or not first:
                        wait(lev_out, t * NL + HP * l + hp)
                    if l == 1 and hp == 0:
                        dve.wait_ge(diag_out, t + 1)
                    if hp == 0:
                        raise_q(t, l)
                    dst = att[:, gs, :, :].rearrange("p g h (n s) -> p (g h) n s", s=2 * s)[:, :, :, s:2 * s]
                    src = ps[:, bank_s[hp], :].rearrange("p (g n s) -> p g n s", n=n, s=s)
                    msk = masks[:, l, :].bitcast(I32).rearrange("p (o n s) -> p o n s", o=1, s=s)
                    nc.vector.copy_predicated(dst, msk.to_broadcast([P, 2 * B, n, s]), src).then_inc(lev_out, 1)

            def diagonal(t):
                dve.wait_ge(lev_out, t * NL + HP)
                wait_alone(dve, diag_done, t + 1)
                src = ps[:, bank_x, 0:2 * G].rearrange("p (g o) -> p g o", o=1)
                msk = ident.bitcast(I32).rearrange("p (o c) -> p o c", o=1)
                nc.vector.copy_predicated(att[:].rearrange("p g h c -> p (g h) c"),
                                          msk.to_broadcast([P, 2 * G, C]),
                                          src.to_broadcast([P, 2 * G, C])).then_inc(diag_out, 1)

            def inverse_roots(t):
                dve.wait_ge(rms_root, t + 1)
                nc.vector.reciprocal(rrms, sroot).then_inc(rrms_done, 1)

            def normed_heads(t, batches):
                dve.wait_ge(rrms_done, t + 1)
                for b in batches:
                    o_h = og[:, b, :].rearrange("p (h n) -> p h n", h=H)
                    sc = rrms[:, b * H:(b + 1) * H].rearrange("p (h o) -> p h o", o=1)
                    nc.vector.tensor_tensor(o_h, o_h, sc.to_broadcast([P, H, HV]), ALU.mult).then_inc(og_ready, 1)

            def lo_o(t, b):
                dve.wait_ge(ogt_hi_out, t * B + b + 1)
                nc.vector.tensor_tensor(ogt_lo[:].rearrange("p h c -> p (h c)"), ps[:, bank_x, :],
                                        ogt_hi[:].bitcast(F32).rearrange("p h c -> p (h c)"),
                                        ALU.subtract).then_inc(ogt_lo_out, 1)

            def residual(t, b, bank=None):
                if b == 0:
                    dve.wait_ge(xtok_in, t * 16 + 16)
                dve.wait_ge(wo_done, t * B + b + 1)
                bank = bank_o[b % 2] if bank is None else bank
                nc.vector.tensor_tensor(y[:, b, :], ps[:, bank, 0:D], xtok[:, b, :],
                                        ALU.add).then_inc(y_out, 1)
                dve.wait_ge(y_out, t * B + b + 1)
                nc.vector.bn_stats(stats[:, b, :], y[:, b, :]).then_inc(st_stats, 1)
                wait_alone(dve, st_stats, t * B + b + 1)
                nc.vector.bn_aggr(mv[:, b, :], stats[:, b, :]).then_inc(st_aggr, 1)

            def var_eps(n_aggr, done, b0=0, b1=B):
                dve.wait_ge(st_aggr, n_aggr)
                nc.vector.tensor_scalar(vare[:, b0:b1], mv[:, b0:b1, 1:2].rearrange("p b o -> p (b o)"), EPS, None,
                                        ALU.add).then_inc(done, 1)

            def norm_rows(src, dst, n_root, root, last_sem, n_rstd, b0=0, b1=B):
                dve.wait_ge(root, n_root)
                nc.vector.reciprocal(rstd[:, b0:b1], sdev[:, b0:b1]).then_inc(rstd_done, 1)
                dve.wait_ge(rstd_done, n_rstd)
                for b in range(b0, b1):
                    op = nc.vector.tensor_scalar(dst(b), src(b), mv[:, b, 0:1], rstd[:, b:b + 1],
                                                 ALU.subtract, ALU.mult)
                op.then_inc(last_sem, 1)

            def finish_x1(t):
                norm_rows(lambda b: y[:, b, :], lambda b: x1_row(t, b), t + 1, ln_root, x1_done, t + 1)

            def neg_gate(t):
                dve.wait_ge(ln_g, t + 1)
                nc.vector.scalar_tensor_tensor(ex[:], gl[:], 0.0, ex[:], ALU.min, ALU.subtract).then_inc(neg_g, 1)

            def heads_out(t, b):
                dve.wait_ge(gw_ready, t * B + b + 1)
                dve.wait_ge(sq_done, t * B + b + 1)
                nc.vector.tensor_tensor(og[:, b, :], ps[:, bank_o[b % 2], :], gate[:, b, :], ALU.mult)
                nc.vector.tensor_reduce(ssum[:, b * H:(b + 1) * H], sq[:].rearrange("p (h n) -> p h n", h=H),
                                        AX, ALU.add).then_inc(o_out, 1)

            def state_out(t, b):
                dve.wait_ge(st_done, t * B + b + 1)
                if b == 0:
                    dve.wait_ge(tot_ready, t * LEVELS + LEVELS)
                for hp in range(HP):
                    g = hp * B + b
                    for par in range(2):
                        rows = slice(par * HK, (par + 1) * HK)
                        s_old = state[rows, g, par, :]
                        add = ps[rows, bank_s[b % 2], (2 * hp + par) * HV:(2 * hp + par + 1) * HV]
                        op = nc.vector.scalar_tensor_tensor(s_old, s_old, total(LEVELS)[rows, g, :], add,
                                                            ALU.mult, ALU.add)
                op.then_inc(st_out, 1)

            def head_means(t):
                dve.wait_ge(o_out, t * B + B)
                nc.vector.tensor_scalar(smean, ssum, 1.0 / HV, EPS, ALU.mult, ALU.add).then_inc(rms_in, 1)

            def x1_lo(t):
                for c in range(KC):
                    dve.wait_ge(tp_hi, t * KC + c + 1)
                    nc.vector.tensor_tensor(x1t_lo[:, c, :], ps[:, 6 + c, :], x1t_hi[:, c, :].bitcast(F32),
                                            ALU.subtract).then_inc(tp_lo, 1)

            def flag():
                dve.wait_ge(checked, NCHECK)
                nc.vector.tensor_reduce(flag_p, unequal, AX, ALU.max).then_inc(flag_local, 1)
                dve.wait_ge(flag_all, 1)
                nc.vector.tensor_scalar(flag_i[:], flag_f, 0.0, None, ALU.is_gt).then_inc(flag_done, 1)

            def look(t, i):
                dve.wait_ge(rounded_done, t * LOOKS + i + 1)
                nc.vector.scalar_tensor_tensor(rounded[:].bitcast(F32), stage[:, i % 2, :], 1.0,
                                               rounded[:].bitcast(F32), ALU.mult, ALU.not_equal,
                                               accum_out=unequal[:, bass.ds(t * LOOKS + i, 1)]).then_inc(checked, 1)

            def tile(t, first=False, last=False):
                if not first:
                    inverse_roots(t - 1)
                level(t, 0, first)
                diagonal(t)
                level(t, 1)
                if last:
                    look(t, 0)
                if not first:
                    lo_o(t - 1, 0)
                for b in range(3):
                    level(t, 2 + b)
                    if not first:
                        residual(t - 1, b)
                        lo_o(t - 1, b + 1)
                    if last:
                        look(t, b + 1)
                level(t, 5)
                if not last:
                    look(t, 0)
                if not first:
                    residual(t - 1, 3)
                    var_eps(t * B, ln_in)
                level(t, 6)
                if last:
                    flag()
                else:
                    dve.wait_ge(g_done, g_vg(t, 8))
                    split_x(t + 1)
                if last:
                    finish_x1(t - 1)
                    heads_out(t, 0)
                    x1_lo(0)
                    heads_out(t, 1)
                    heads_out(t, 2)
                    heads_out(t, 3)
                    head_means(t)
                    return
                if not first:
                    finish_x1(t - 1)
                heads_out(t, 0)
                state_out(t, 0)
                look(t, 1)
                heads_out(t, 1)
                state_out(t, 1)
                look(t, 2)
                neg_gate(t + 1)
                look(t, 3)
                heads_out(t, 2)
                state_out(t, 2)
                dve.wait_ge(o_done, t * B + B)
                start_q(t + 1, 0, g_next(t, 4))
                state_out(t, 3)
                start_q(t + 1, 1, g_next(t, 5))
                heads_out(t, 3)
                head_means(t)

            dve.wait_ge(gates_in, 3 * 16)
            dve.wait_ge(zeroed, 1)
            nc.vector.tensor_copy(gk1_hi[:, :, 0:LR], raw_gk1).then_inc(gk1_split, 1)
            dve.wait_ge(gk1_split, 1)
            nc.vector.tensor_tensor(gk1_lo[:, :, 0:LR], raw_gk1, gk1_hi[:, :, 0:LR].bitcast(F32),
                                    ALU.subtract).then_inc(gk1_split, 1)
            split_x(0)
            dve.wait_ge(wqk_in, 16)
            nc.vector.tensor_copy(wa_hi[:, :, 0:2 * D], raw_attn[:, :, 0:2 * D]).then_inc(w_hi, 1)
            dve.wait_ge(w_hi, 1)
            nc.vector.tensor_tensor(wa_lo[:, :, 0:2 * D], raw_attn[:, :, 0:2 * D],
                                    wa_hi[:, :, 0:2 * D].bitcast(F32), ALU.subtract).then_inc(w_split, 1)
            dve.wait_ge(wrest_in, 32)
            nc.vector.tensor_copy(wa_hi[:, :, 2 * D:], raw_attn[:, :, 2 * D:]).then_inc(w_hi, 1)
            nc.vector.tensor_copy(wo_hi[:], raw_o).then_inc(w_hi, 1)
            dve.wait_ge(w_hi, 3)
            nc.vector.tensor_tensor(wa_lo[:, :, 2 * D:], raw_attn[:, :, 2 * D:],
                                    wa_hi[:, :, 2 * D:].bitcast(F32), ALU.subtract)
            nc.vector.tensor_tensor(wo_lo[:], raw_o, wo_hi[:].bitcast(F32), ALU.subtract).then_inc(w_split, 1)
            neg_gate(0)
            dve.wait_ge(zeroed, 4)
            start_q(0, 0, 4)
            start_q(0, 1, 5)
            dve.wait_ge(consts_in, 5 * 16)
            tile(0, first=True)
            with dve.Fori(1, NT - 1) as t:
                tile(t)
            tile(NT - 1, last=True)
            def lo_part(t, layer, m):
                dst = (ha_lo, hb_lo, ha_lo)[layer]
                hi = (ha_hi, hb_hi, ha_hi)[layer]
                if layer == 0:
                    dve.wait_ge(hi1_ready, t * MC + m + 1)
                else:
                    n = t * 2 * MC + (layer - 1) * MC + m + 1
                    dve.wait_ge(gelu_done, n)
                    nc.vector.tensor_copy(hi[:, m, :], hf[:, m % 2, :]).then_inc(hi23_ready, 1)
                    dve.wait_ge(hi23_ready, n)
                nc.vector.tensor_tensor(dst[:, m, :], hf[:, m % 2, :], hi[:, m, :].bitcast(F32),
                                        ALU.subtract).then_inc(lo_ready, 1)

            def last_heads_lo(b):
                dve.wait_ge(ogt_hi_out, (NT - 1) * B + b + 1)
                nc.vector.tensor_tensor(ogt_lo[:].rearrange("p h c -> p (h c)"), ps[:, bank_o[0], :],
                                        ogt_hi[:].bitcast(F32).rearrange("p h c -> p (h c)"),
                                        ALU.subtract).then_inc(ogt_lo_out, 1)

            def norm_y2(t):
                norm_rows(lambda b: xcur[:, b, :], lambda b: x1_row(t, b), t + 1, ln2_root, y2_ready, t + (NT + 1))

            def norm_last(i):
                b0, b1 = HALVES[i]
                norm_rows(lambda b: xcur[:, b, :], lambda b: x1_row(NT - 1, b), NT + i, ln2_root, y2_ready,
                          2 * NT + i, b0, b1)

            def ffn_tile(t, first=False, last=False):
                if first:
                    inverse_roots(NT - 1)
                    normed_heads(NT - 1, (0, 1))
                for m in range(MC):
                    if first and m >= 4:
                        residual(NT - 1, m - 4, bank_o[1])
                    if first and m in (2, 4, 5, 6):
                        last_heads_lo(m - 3 if m > 2 else 0)
                    dve.wait_ge(sil_done, t * MC + m + 1)
                    if m >= 2 or not first:
                        dve.wait_ge(lo_ready, t * 3 * MC + m - 1)
                    nc.vector.scalar_tensor_tensor(hf[:, m % 2, :], ps[:, pair_1[m % 3] + 1, :],
                                                   scales[:, 1, m:m + 1], sil[:, m % 2, :], ALU.mult,
                                                   ALU.mult).then_inc(ha_ready, 1)
                    if m:
                        lo_part(t, 0, m - 1)
                    if first and m < 2:
                        normed_heads(NT - 1, (m + 2,))
                lo_part(t, 0, MC - 1)
                if first:
                    var_eps(NT * B, ln_in)
                    finish_x1(NT - 1)
                    dve.wait_ge(x1_done, NT)
                else:
                    norm_y2(t - 1)
                for layer in (1, 2):
                    for m in range(MC):
                        lo_part(t, layer, m)
                if not last:
                    x1_lo(t + 1)
                for b in range(B):
                    dve.wait_ge(f4_done, t * B + b + 1)
                    nc.vector.tensor_tensor(xcur[:, b, :], ps[:, 4 + b % 2, 0:D], w3s[:],
                                            ALU.mult).then_inc(f4_out, 1)
                    dve.wait_ge(f4_out, t * B + b + 1)
                    nc.vector.tensor_tensor(xcur[:, b, :], xcur[:, b, :], x1_row(t, b), ALU.add).then_inc(res2, 1)
                    dve.wait_ge(res2, t * B + b + 1)
                    nc.vector.bn_stats(stats[:, b, :], xcur[:, b, :]).then_inc(st_stats, 1)
                    wait_alone(dve, st_stats, t * B + (NT * B + b + 1))
                    nc.vector.bn_aggr(mv[:, b, :], stats[:, b, :]).then_inc(st_aggr, 1)
                    if last and b + 1 in (B // 2, B):
                        b0, b1 = HALVES[b // (B // 2)]
                        var_eps(t * B + (NT * B + b + 1), ln2_in, b0, b1)
                    if last and b == B // 2:
                        norm_last(0)
                if not last:
                    var_eps(t * B + (NT * B + B), ln2_in)

            ffn_tile(0, first=True)
            with dve.Fori(1, NT - 1) as t:
                ffn_tile(t)
            ffn_tile(NT - 1, last=True)
            norm_last(1)

        @block.gpsimd
        def _(pool):
            nc.gpsimd.memset(kt[:, 0:B, :], 0.0).then_inc(warm_ready, 1)
            nc.gpsimd.memset(gk1_hi[:].bitcast(F32), 0.0)
            nc.gpsimd.memset(gk1_lo[:].bitcast(F32), 0.0).then_inc(zeroed, 1)
            nc.gpsimd.memset(q2[:], 0.0).then_inc(zeroed, 1)
            nc.gpsimd.memset(att[:], 0.0).then_inc(zeroed, 1)
            nc.gpsimd.memset(state[:], 0.0).then_inc(zeroed, 1)
            pool.wait_ge(consts_in, 5 * 16)

            def totals(t, l):
                if l == 1:
                    pool.wait_ge(decay_ready, t + 1)
                else:
                    pool.wait_ge(tot_ready, t * LEVELS + (l - 1))
                pairs = total(l - 1).rearrange("p g (n two) -> p g n two", two=2)
                dst = total(l).rearrange("p g (n o) -> p g n o", o=1)
                nc.gpsimd.tensor_tensor(dst, pairs[:, :, :, 0:1], pairs[:, :, :, 1:2],
                                        ALU.mult).then_inc(tot_ready, 1)

            def level(t, l, last):
                s = 1 << l
                n = C // (2 * s)
                halves = total(l).rearrange("p g (n two) -> p g n two", two=2)
                k_left = k[:].rearrange("p g (n s) -> p g n s", s=2 * s)[:, :, :, 0:s]
                for hp in range(HP):
                    gs = slice(hp * B, (hp + 1) * B)
                    pool.wait_ge(lev_done, t * NL + HP * l + hp + 1)
                    if l:
                        pool.wait_ge(tot_ready, t * LEVELS + l)
                    else:
                        pool.wait_ge(qk_ready, t + 1)
                    if hp == 1:
                        pool.wait_ge(q_ready[1], t * NQ + l + 1)
                        for par in range(2):
                            q_right = q2[:, gs, par, :].rearrange("p g (n s) -> p g n s", s=2 * s)[:, :, :, s:2 * s]
                            op = nc.gpsimd.tensor_tensor(q_right, q_right,
                                                         halves[:, gs, :, 0:1].to_broadcast([P, B, n, s]), ALU.mult)
                        op.then_inc(q_ready[1], 1)
                    if last and l == LEVELS - 1:
                        continue
                    if l:
                        pool.wait_ge(k_ready, t * NL + HP * (l - 1) + hp + 1)
                    nc.gpsimd.tensor_tensor(k_left[:, gs], k_left[:, gs],
                                            halves[:, gs, :, 1:2].to_broadcast([P, B, n, s]),
                                            ALU.mult).then_inc(k_ready, 1)

            def tile(t, last=False):
                totals(t, 1)
                pool.wait_ge(g_out, t * NG + 7)
                pool.wait_ge(decay_ready, t + 1)
                nc.gpsimd.tensor_tensor(qk[:], q[:], k[:], ALU.mult).then_inc(qk_ready, 1)
                for l in range(LEVELS):
                    level(t, l, last)
                    if l + 2 <= LEVELS - last:
                        totals(t, l + 2)
                if last:
                    pool.wait_ge(flag_local, 1)
                    nc.gpsimd.partition_all_reduce(flag_f, flag_p, P, bass.bass_isa.ReduceOp.max).then_inc(flag_all, 1)
                for b in range(B):
                    pool.wait_ge(g_out, g_vg(t, 4 + b) + 1)
                    g_h = gate[:, b, :].rearrange("p (h n) -> p h n", h=H)
                    w_h = rms[:].rearrange("p (o n) -> p o n", o=1)
                    nc.gpsimd.tensor_tensor(g_h, g_h, w_h.to_broadcast([P, H, HV]), ALU.mult).then_inc(gw_ready, 1)

            with pool.Fori(0, NT - 1) as t:
                tile(t)
            tile(NT - 1, last=True)

            def copy_x1(t):
                nc.gpsimd.tensor_copy(xcur[:].rearrange("p b d -> p (b d)"), x1_tile(t)).then_inc(xcur_ready, 1)

            wait_alone(pool, x1_done, 2)
            copy_x1(1)
            with pool.Fori(2, NT) as t:
                wait_alone(pool, y2_ready, t - 1)
                copy_x1(t)


_OUTS = [((B, T, D), "float32")]


def kernel(**inputs):
    import concourse.bacc as _bacc
    from concourse.bass_utils import run_bass_kernel_spmd as _run

    a = {n: np.ascontiguousarray(v) for n, v in inputs.items()}

    def rows(w, chunks):
        return w.reshape(chunks, P, -1).transpose(1, 0, 2)

    x = a["L0_attn_x"]
    attn = rows(np.concatenate([a["L0_attn_Wq"], a["L0_attn_Wk"], a["L0_attn_Wv"], a["L0_attn_Wg"]], axis=1), KC)
    flat = lambda w: w.reshape(P, -1)
    consts = np.zeros((P, P + 2), np.float32)
    consts[:, :P] = np.eye(P, dtype=np.float32)
    consts[:HK, -2] = 1.0
    consts[HK:, -1] = 1.0
    sent = {
        "x": x,
        "xT": x.reshape(B, NT, C, KC, P).transpose(1, 4, 3, 0, 2).reshape(NT, P, KC, TOK),
        "w_attn": attn,
        "w_o": rows(a["L0_attn_Wo"], H),
        "gk1": rows(a["L0_attn_gk_w1"], KC),
        "gk2": a["L0_attn_gk_w2"],
        "gk_b": a["L0_attn_gk_b"].reshape(HP, P).T,
        "rms_w": a["L0_attn_rms_w"],
        "w123": np.concatenate([flat(rows(a["L0_ffn_w1_w"].T, KC)), flat(rows(a["L0_ffn_w2_w"].T, KC)),
                                flat(rows(a["L0_ffn_w3_w"].T, MC))], axis=1),
        "wh1": flat(rows(a["L0_ffn_h1_w"].T, MC)),
        "wh2": flat(rows(a["L0_ffn_h2_w"].T, MC)),
        "s_in": np.stack([a[f"L0_ffn_{n}_s"].reshape(MC, P).T for n in ("w1", "w2", "h1", "h2")], axis=1),
        "w3_s": a["L0_ffn_w3_s"],
        "consts": consts,
        "level_mask": level_masks(),
    }
    nc = _bacc.Bacc("TRN2", target_bir_lowering=False, num_devices=1)
    arrays, args = {}, []
    for name, v in sent.items():
        v = np.ascontiguousarray(v)
        arrays[f"in_{name}"] = v
        args.append(nc.dram_tensor(f"in_{name}", v.shape, mybir.dt.from_np(v.dtype), kind="ExternalInput").ap())
    for i, (shape, dtype) in enumerate(_OUTS):
        args.append(nc.dram_tensor(f"out_{i}", shape, mybir.dt.from_np(np.dtype(dtype)), kind="ExternalOutput").ap())
    build(nc, *args)
    r = _run(nc, [arrays], core_ids=[0])
    return r.results[0]["out_0"]
```
